# Optimizing a Trainium2 kernel written in Bass

```python
import numpy as np
import jax
import jax.numpy as jnp

def _softmax(x, axis=-1):
    return jax.nn.softmax(x, axis=axis)

def _gelu(x):
    return jax.nn.gelu(x, approximate=True)

def _silu(x):
    return jax.nn.silu(x)

def _sigmoid(x):
    return jax.nn.sigmoid(x)

def _layernorm(x, axis=-1, eps=1e-05):
    m = jnp.mean(x, axis=axis, keepdims=True)
    v = jnp.var(x, axis=axis, keepdims=True)
    return (x - m) / jnp.sqrt(v + eps)

def _scatter_add(tgt, idx, src, axis=0):
    return tgt.at[idx].add(src)

def _segment_sum(src, seg, n):
    return jax.ops.segment_sum(src, seg, n)
kernel_name = 'mk_adj_preln_d4_adj_r2_d17e3f'

def setup_inputs(seed: int=0):
    np.random.seed(seed)
    _w = jnp.asarray

    def _rec_inputs():
        import jax
        import jax.numpy as jnp
        _gk = jax.random.key(seed)
        x = -0.0002928 + 1 * jax.random.normal(jax.random.fold_in(_gk, 1), (16, 512, 256), jnp.float32)
        _a = jax.random.bernoulli(jax.random.fold_in(_gk, 2), 0.015625, (16, 512, 512))
        _a = jnp.logical_or(_a, jnp.swapaxes(_a, -1, -2))
        _a = jnp.logical_or(_a, jnp.eye(512, dtype=bool))
        adj = _a.astype(jnp.int32)
        return (x, adj)
    x, adj = _rec_inputs()

    def _L0_gnn_setup():
        import jax, jax.numpy as jnp
        import numpy as np
        B, N, D = (8, 512, 256)
        NH = 8
        DK = D // NH
        key = jax.random.key(seed)
        ks = jax.random.split(key, 6)
        x = jax.random.normal(ks[0], (B, N, D), dtype=jnp.float32)
        adj = jax.random.randint(ks[1], (B, N, N), 0, 2, dtype=jnp.int32)
        adj = jnp.maximum(adj, jnp.eye(N, dtype=jnp.int32)[None])
        s = 1.0 / np.sqrt(D)
        Wq = jax.random.normal(ks[2], (D, D), dtype=jnp.float32) * s
        Wk = jax.random.normal(ks[3], (D, D), dtype=jnp.float32) * s
        Wv = jax.random.normal(ks[4], (D, D), dtype=jnp.float32) * s
        Wo = jax.random.normal(ks[5], (D, D), dtype=jnp.float32) * s
        return {'x': x, 'adj': adj, 'Wq': Wq, 'Wk': Wk, 'Wv': Wv, 'Wo': Wo}
    _L0_gnn_all = _L0_gnn_setup()
    _L0_gnn_in = {k: v for k, v in _L0_gnn_all.items() if k in ('Wq', 'Wk', 'Wv', 'Wo')}
    del _L0_gnn_all

    def _L1_gnn_setup():
        import jax, jax.numpy as jnp
        import numpy as np
        L = 3
        D = 256
        B, N = (8, 512)
        EPS = 1e-05

        def layernorm(x, gamma, beta):
            mu = jnp.mean(x, axis=-1, keepdims=True)
            var = jnp.var(x, axis=-1, keepdims=True)
            return (x - mu) * jax.lax.rsqrt(var + EPS) * gamma + beta
        key = jax.random.key(seed)
        ks = jax.random.split(key, 12)
        s = 1.0 / np.sqrt(D)
        node_features = jax.random.normal(ks[0], (B, N, D), dtype=jnp.float32)
        adjacency_matrix = jax.random.randint(ks[1], (B, N, N), 0, 2, dtype=jnp.int32)
        return {'node_features': node_features, 'adjacency_matrix': adjacency_matrix, 'attn_w': jax.random.normal(ks[2], (L, 2 * D), dtype=jnp.float32) * (1.0 / np.sqrt(2 * D)), 'attn_b': jax.random.normal(ks[3], (L,), dtype=jnp.float32) * 0.01, 'W1': jax.random.normal(ks[4], (L, D, 4 * D), dtype=jnp.float32) * s, 'b1': jnp.zeros((L, 4 * D), dtype=jnp.float32), 'W2': jax.random.normal(ks[5], (L, 4 * D, D), dtype=jnp.float32) * (1.0 / np.sqrt(4 * D)), 'b2': jnp.zeros((L, D), dtype=jnp.float32), 'g1': jnp.ones((L, D), dtype=jnp.float32), 'beta1': jnp.zeros((L, D), dtype=jnp.float32), 'g2': jnp.ones((L, D), dtype=jnp.float32), 'beta2': jnp.zeros((L, D), dtype=jnp.float32)}
    _L1_gnn_all = _L1_gnn_setup()
    _L1_gnn_in = {k: v for k, v in _L1_gnn_all.items() if k in ('attn_w', 'attn_b', 'W1', 'b1', 'W2', 'b2', 'g1', 'beta1', 'g2', 'beta2')}
    del _L1_gnn_all

    def _L2_gnn_setup():
        import jax, jax.numpy as jnp
        import numpy as np
        B, N, DIN, DOUT = (8, 1024, 256, 256)
        key = jax.random.key(seed)
        kx, ka, kw, kb, kattn = jax.random.split(key, 5)
        x = jax.random.normal(kx, (B, N, DIN), dtype=jnp.float32)
        adjacency_matrix = jax.random.randint(ka, (B, N, N), 0, 2, dtype=jnp.int32)
        lim_w = float(np.sqrt(1.0 / DIN))
        W = jax.random.uniform(kw, (DOUT, DIN), minval=-lim_w, maxval=lim_w, dtype=jnp.float32)
        b = jax.random.uniform(kb, (DOUT,), minval=-lim_w, maxval=lim_w, dtype=jnp.float32)
        lim_a = float(np.sqrt(6.0 / (DOUT + DOUT)))
        attn = jax.random.uniform(kattn, (DOUT, DOUT), minval=-lim_a, maxval=lim_a, dtype=jnp.float32)
        return {'x': x, 'adjacency_matrix': adjacency_matrix, 'W': W, 'b': b, 'attn': attn}
    _L2_gnn_all = _L2_gnn_setup()
    _L2_gnn_in = {k: v for k, v in _L2_gnn_all.items() if k in ('W', 'b', 'attn')}
    del _L2_gnn_all

    def _L3_gnn_setup():
        import jax, jax.numpy as jnp
        import numpy as np
        ALPHA = 0.2
        MASK_VAL = -1000000000.0
        key = jax.random.key(seed)
        k1, k2, k3, k4 = jax.random.split(key, 4)
        B, N, F_in, F_out = (8, 1024, 256, 256)
        h = jax.random.normal(k1, (B, N, F_in), dtype=jnp.float32)
        adj = jax.random.randint(k2, (B, N, N), 0, 2, dtype=jnp.int32)

        def xavier(k, shape, gain=1.414):
            fan_in, fan_out = (shape[0], shape[1])
            bound = gain * np.sqrt(6.0 / (fan_in + fan_out))
            return jax.random.uniform(k, shape, jnp.float32, -bound, bound)
        W = xavier(k3, (F_in, F_out))
        a = xavier(k4, (2 * F_out, 1))
        return {'h': h, 'adj': adj, 'W': W, 'a': a}
    _L3_gnn_all = _L3_gnn_setup()
    _L3_gnn_in = {k: v for k, v in _L3_gnn_all.items() if k in ('W', 'a')}
    del _L3_gnn_all
    return {'x': x, 'adj': adj, 'L0_gnn_Wq': _L0_gnn_in['Wq'], 'L0_gnn_Wk': _L0_gnn_in['Wk'], 'L0_gnn_Wv': _L0_gnn_in['Wv'], 'L0_gnn_Wo': _L0_gnn_in['Wo'], 'L1_gnn_attn_w': _L1_gnn_in['attn_w'], 'L1_gnn_attn_b': _L1_gnn_in['attn_b'], 'L1_gnn_W1': _L1_gnn_in['W1'], 'L1_gnn_b1': _L1_gnn_in['b1'], 'L1_gnn_W2': _L1_gnn_in['W2'], 'L1_gnn_b2': _L1_gnn_in['b2'], 'L1_gnn_g1': _L1_gnn_in['g1'], 'L1_gnn_beta1': _L1_gnn_in['beta1'], 'L1_gnn_g2': _L1_gnn_in['g2'], 'L1_gnn_beta2': _L1_gnn_in['beta2'], 'L2_gnn_W': _L2_gnn_in['W'], 'L2_gnn_b': _L2_gnn_in['b'], 'L2_gnn_attn': _L2_gnn_in['attn'], 'L3_gnn_W': _L3_gnn_in['W'], 'L3_gnn_a': _L3_gnn_in['a']}

def reference(x, adj, L0_gnn_Wq, L0_gnn_Wk, L0_gnn_Wv, L0_gnn_Wo, L1_gnn_attn_w, L1_gnn_attn_b, L1_gnn_W1, L1_gnn_b1, L1_gnn_W2, L1_gnn_b2, L1_gnn_g1, L1_gnn_beta1, L1_gnn_g2, L1_gnn_beta2, L2_gnn_W, L2_gnn_b, L2_gnn_attn, L3_gnn_W, L3_gnn_a):
    import jax
    import jax.numpy as jnp

    def _L0_gnn_ref(x, adj, Wq, Wk, Wv, Wo):
        import jax, jax.numpy as jnp
        import numpy as np
        B, N, D = (8, 512, 256)
        NH = 8
        DK = D // NH
        b, n, d = x.shape
        sqrt_dk = jnp.asarray(np.sqrt(DK), dtype=x.dtype)

        def heads(t):
            return t.reshape(b, n, NH, DK).transpose(0, 2, 1, 3)
        q = heads(x @ Wq)
        k = heads(x @ Wk)
        v = heads(x @ Wv)
        scores = jnp.einsum('bhnd,bhmd->bhnm', q, k) / sqrt_dk
        mask = adj.astype(bool)[:, None]
        scores = jnp.where(mask, scores, -jnp.inf)
        attn = jax.nn.softmax(scores, axis=-1)
        out = jnp.einsum('bhnm,bhmd->bhnd', attn, v)
        out = out.transpose(0, 2, 1, 3).reshape(b, n, d)
        return jax.nn.relu(out) @ Wo

    def _L1_gnn_ref(node_features, adjacency_matrix, attn_w, attn_b, W1, b1, W2, b2, g1, beta1, g2, beta2):
        import jax, jax.numpy as jnp
        import numpy as np
        L = 3
        D = 256
        B, N = (8, 512)
        EPS = 1e-05

        def layernorm(x, gamma, beta):
            mu = jnp.mean(x, axis=-1, keepdims=True)
            var = jnp.var(x, axis=-1, keepdims=True)
            return (x - mu) * jax.lax.rsqrt(var + EPS) * gamma + beta
        n = adjacency_matrix.shape[-1]
        mask = adjacency_matrix.astype(jnp.float32) + jnp.eye(n, dtype=jnp.float32) > 0
        x = node_features
        d = x.shape[-1]
        for l in range(attn_w.shape[0]):
            si = x @ attn_w[l, :d]
            sj = x @ attn_w[l, d:]
            scores = si[:, :, None] + sj[:, None, :] + attn_b[l]
            scores = jnp.where(scores >= 0, scores, 0.2 * scores)
            scores = jnp.where(mask, scores, -jnp.inf)
            attn = jax.nn.softmax(scores, axis=-1)
            agg = jnp.einsum('bij,bjd->bid', attn, x)
            h = layernorm(x + agg, g1[l], beta1[l])
            ff = jax.nn.gelu(h @ W1[l] + b1[l], approximate=False) @ W2[l] + b2[l]
            x = layernorm(h + ff, g2[l], beta2[l])
        return x

    def _L2_gnn_ref(x, adjacency_matrix, W, b, attn):
        import jax, jax.numpy as jnp
        import numpy as np
        B, N, DIN, DOUT = (8, 1024, 256, 256)
        h = jnp.einsum('bni,oi->bno', x, W) + b
        ha = jnp.einsum('bmi,ij->bmj', h, attn)
        scores = jnp.einsum('bmj,bnj->bmn', ha, h)
        scores = jnp.where(adjacency_matrix == 0, -jnp.inf, scores)
        attn_weights = jax.nn.softmax(scores, axis=-1)
        x_out = jnp.einsum('bmn,bnd->bmd', attn_weights, h)
        return jax.nn.elu(x_out)

    def _L3_gnn_ref(h, adj, W, a):
        import jax, jax.numpy as jnp
        import numpy as np
        ALPHA = 0.2
        MASK_VAL = -1000000000.0
        Fout = W.shape[1]
        Wh = jnp.matmul(h, W)
        a1 = a[:Fout, 0]
        a2 = a[Fout:, 0]
        e_i = jnp.einsum('bnf,f->bn', Wh, a1)
        e_j = jnp.einsum('bnf,f->bn', Wh, a2)
        e = e_i[:, :, None] + e_j[:, None, :]
        e = jax.nn.leaky_relu(e, negative_slope=ALPHA)
        e = jnp.where(adj == 0, MASK_VAL, e)
        attention = jax.nn.softmax(e, axis=2)
        h_prime = jnp.matmul(attention, Wh)
        return jax.nn.elu(h_prime)
    h = jnp.maximum(_layernorm(x, axis=-1), 0.0)
    x = x + _L0_gnn_ref(h, adj, L0_gnn_Wq, L0_gnn_Wk, L0_gnn_Wv, L0_gnn_Wo)
    h = jnp.maximum(_layernorm(x, axis=-1), 0.0)
    x = x + _L1_gnn_ref(h, adj, L1_gnn_attn_w, L1_gnn_attn_b, L1_gnn_W1, L1_gnn_b1, L1_gnn_W2, L1_gnn_b2, L1_gnn_g1, L1_gnn_beta1, L1_gnn_g2, L1_gnn_beta2)
    h = jnp.maximum(_layernorm(x, axis=-1), 0.0)
    x = x + _L2_gnn_ref(h, adj, L2_gnn_W, L2_gnn_b, L2_gnn_attn)
    h = jnp.maximum(_layernorm(x, axis=-1), 0.0)
    x = x + _L3_gnn_ref(h, adj, L3_gnn_W, L3_gnn_a)
    return x

_drawn_inputs = setup_inputs


def setup_inputs(seed=0):
    import zlib

    import numpy as np

    out = dict(_drawn_inputs(seed))
    spreads = {'L1_gnn_b1': (0.0, 0.1),
     'L1_gnn_b2': (0.0, 0.1),
     'L1_gnn_g1': (1.0, 0.2),
     'L1_gnn_beta1': (0.0, 0.1),
     'L1_gnn_g2': (1.0, 0.2),
     'L1_gnn_beta2': (0.0, 0.1)}
    factors = {'L1_gnn_attn_b': 200.0, 'L2_gnn_b': 2.989}
    for name, (base, spread) in spreads.items():
        noise = np.random.default_rng([zlib.crc32(name.encode()), seed]).standard_normal(out[name].shape)
        drawn = base * np.exp(spread * noise) if base else spread * noise
        out[name] = jnp.asarray(drawn.astype(out[name].dtype))
    for name, factor in factors.items():
        out[name] = (out[name] * factor).astype(out[name].dtype)
    return out
```

```python
from contextlib import ExitStack

import concourse.bass as bass
from concourse import mybir

F32 = mybir.dt.float32
F16 = mybir.dt.float16
BF16 = mybir.dt.bfloat16
I32 = mybir.dt.int32
ALU = mybir.AluOpType
ACT = mybir.ActivationFunctionType

P = 128
B, N, D = 16, 512, 256
NT = N // P
ND = D // P
NH, DK = 8, 32
HG = P // DK
L1N = 3
HID = 4 * D
NC = HID // P
EPS = 1e-5
MASKED = -1e30
NEG_SCALE = -float(DK) ** -0.5
SLOPE = 0.2
STREAMS = 2

W_L0, W_TAIL, W_UP, W_DOWN = 0, 1, 2, 5
NBLK = 8
USE_L2, USE_L3 = 3, 4
TURN_OF = {0: 0, 2: 1, 4: 2, 6: 3, 8: 4, 9: 5}


def build(nc, x, adj, Wq, Wk, Wv, Wo, attn_w, attn_b, W1, b1, W2, b2, g1, beta1, g2, beta2,
          L2W, L2b, L2attn, L3W, L3a, out):
    ctx = ExitStack()
    with ctx:
        def sb(name, shape, dt):
            return ctx.enter_context(nc.sbuf_tensor(name, shape, dt))

        WH = sb("weights_hi", [P, NBLK, 2048], F16)
        WL = sb("weights_lo", [P, NBLK, 2048], F16)
        ident = sb("ident", [P, P], F32)
        ones = sb("ones", [P, P], F32)
        minus_half = sb("minus_half", [P, NT], F32)
        g1_bc = sb("g1_bc", [P, L1N, D], F32)
        res_bc = sb("beta1_b2_bc", [P, L1N, D], F32)
        g2_bc = sb("g2_bc", [P, L1N, D], F32)
        beta2_bc = sb("beta2_bc", [P, L1N, D], F32)
        a_bc = sb("a_bc", [P, L1N + 1, 2, D], F32)
        ab_bc = sb("attn_b_bc", [P, L1N + 1], F32)
        g1_col = sb("g1_col", [P, L1N, ND], F32)
        beta1_col = sb("beta1_col", [P, L1N, ND], F32)
        b1_col = sb("b1_col", [P, L1N, NC], F32)
        l2b_col = sb("l2b_col", [P, ND], F32)
        X = [sb(f"x{s}", [P, NT, D], F32) for s in range(2)]
        mask = [sb(f"mask{s}", [P, NT, NT, P], BF16) for s in range(2)]
        mask_self = [sb(f"mask_self{s}", [P, NT, NT, P], BF16) for s in range(2)]
        Y = sb("y", [P, NT, D], F32)
        hT_hi = [sb(f"hT_hi{s}", [P, ND, N], F16) for s in range(2)]
        hT_lo = [sb(f"hT_lo{s}", [P, ND, N], F16) for s in range(2)]
        tT = sb("tT", [P, ND, N], F32)
        Z = sb("z", [P, NT, N], F32)
        PR = sb("probs", [P, 3, NT, N], F32)
        V = tT[:, :, :].rearrange("p c (a d) -> p (c a) d", a=2)
        arena = sb("arena", [P, 12288], F32)
        PT = arena[:, 0:8192].rearrange("p (h j n) -> p h j n", h=HG, j=NT)
        ST = arena[:, 0:2048].bitcast(F16).rearrange("p (w m e n) -> p w m e n", w=2, m=2, e=2)
        QS = arena[:, 8192:10240].bitcast(F16).rearrange("p (h n) -> p h n", h=NH)
        KS = arena[:, 10240:12288].bitcast(F16).rearrange("p (h n) -> p h n", h=NH)
        XN = [arena[:, 1024 * s:1024 * s + 1024].rearrange("p (t d) -> p t d", t=NT) for s in range(2)]
        RES = [arena[:, 2048 + 1024 * s:3072 + 1024 * s].rearrange("p (t d) -> p t d", t=NT) for s in range(2)]
        XH = [arena[:, 4096 + 1024 * s:4608 + 1024 * s].bitcast(F16).rearrange("p (t d) -> p t d", t=NT) for s in range(2)]
        XL = [arena[:, 4608 + 1024 * s:5120 + 1024 * s].bitcast(F16).rearrange("p (t d) -> p t d", t=NT) for s in range(2)]
        PTH = arena[:, 6144:7168].bitcast(F16).rearrange("p (j n) -> p j n", j=NT)
        PTL = arena[:, 7168:8192].bitcast(F16).rearrange("p (j n) -> p j n", j=NT)
        GF = arena[:, 8192:9216].rearrange("p (r n) -> p r n", r=2)
        GH = arena[:, 9216:9728].bitcast(F16).rearrange("p (r n) -> p r n", r=2)
        GL = arena[:, 9728:10240].bitcast(F16).rearrange("p (r n) -> p r n", r=2)
        HAH = arena[:, 10240:10752].bitcast(F16).rearrange("p (m n) -> p m n", m=ND)
        HAL = arena[:, 10752:11264].bitcast(F16).rearrange("p (m n) -> p m n", m=ND)
        diag = arena[:, 11264:11776].rearrange("p (t n) -> p t n", t=NT)
        NMIN = sb("nmin", [P, 2, NH, NT], F32)
        RSUM = sb("rsum", [P, 2, NH, NT], F32)
        RINV = sb("rinv", [P, 2, NH, NT], F32)
        stats = sb("stats", [P, NT, 6], F32)
        mv = sb("mv", [P, NT, 2], F32)
        ve = sb("ve", [P, NT], F32)
        rstd = sb("rstd", [P, NT], F32)
        sml = sb("small", [P, 8, NT], F32)
        eb = sb("eb", [P, 2, 2, NT], F32)
        U = [ctx.enter_context(nc.psum_tensor(f"U{i}", [P, 512], F32)) for i in range(2)]
        YB = [ctx.enter_context(nc.psum_tensor(f"Y{i}", [P, 512], F32)) for i in range(2)]
        PB = [ctx.enter_context(nc.psum_tensor(f"P{i}", [P, 512], F32)) for i in range(2)]
        GB = [ctx.enter_context(nc.psum_tensor(f"G{i}", [P, 512], F32)) for i in range(2)]
        SB4 = [PB[0], PB[1], GB[0], GB[1]]

        def sem(name):
            return ctx.enter_context(nc.semaphore(name))

        def per_stream(name):
            return [sem(f"{name}{s}") for s in range(STREAMS)]

        loaded = [sem(f"loaded{i}") for i in range(NBLK)]
        split, wT = sem("split"), sem("wT")
        const_ready, ident_ready = sem("const_ready"), sem("ident_ready")
        x_in, adj_in = per_stream("x_in"), per_stream("adj_in")
        mask_ready, self_ready = per_stream("mask_ready"), per_stream("self_ready")
        stat_done, aggr_done, var_ready, rstd_ready = (per_stream(n) for n in ("stat", "aggr", "var", "rstd"))
        y_ready, yT_ready, hi_ready, lo_ready, t_ready = (per_stream(n) for n in ("y", "yT", "hT_hi", "hT_lo", "tT"))
        qk_ps, qk_hi, qk_lo = per_stream("qk_ps"), per_stream("qk_hi"), per_stream("qk_lo")
        stack_in = [[sem(f"stack{m}_{s}") for s in range(2)] for m in range(2)]
        v_ps, v_ready = per_stream("v_ps"), per_stream("v_sb")
        s0_ready, z0_ready, p0_ready, r0_ready, pn_ready, pt0_ps, pt0_act, pt0_dve, pv_done = (
            per_stream(n) for n in ("s0", "z0", "p0", "r0", "pn", "pt0", "pt0_act", "pt0_dve", "pv"))
        o_hi, o_lo, wo_done, x1_ready = (per_stream(n) for n in ("o_hi", "o_lo", "wo", "x1"))
        dot_done, diag_ready, sj_ready, z_ready, small_done, small_ready = (
            per_stream(n) for n in ("dot", "diag", "sj", "z", "small", "bias"))
        relu_ready, w_ready, p_ready, pt_ps, pt_hi, pt_lo, agg_ps, rinv_ready = (
            per_stream(n) for n in ("relu", "w", "p", "pt", "pt_hi", "pt_lo", "agg", "rinv"))
        xn_ready, xhi_ready, xlo_ready, src_ready, res_half, res_ready = (
            per_stream(n) for n in ("xn", "x_hi", "x_lo", "src", "res_half", "res"))
        up_ps, g_ready, glo_ready, down_done = (per_stream(n) for n in ("up", "g", "g_lo", "down"))
        h2_ps, h2_f, h2_lo, ha_ps, ha_hi, ha_lo, hn_ps, s2_ps = (
            per_stream(n) for n in ("h2_ps", "h2_f", "h2_lo", "ha_ps", "ha_hi", "ha_lo", "hn_ps", "s2"))
        hp_ready, mn_ready, ex_ready, el_ready, xs_ready = (per_stream(n) for n in ("hp", "mn", "ex", "el", "xs"))
        half_done = per_stream("x_half")
        stored = per_stream("stored")
        sems = range(loaded[0].num, stored[-1].num + 1)

        stage = [Z[:, :, :].rearrange("p t n -> p (t n)"), PR[:, 0, :, :].rearrange("p t n -> p (t n)")]

        def bcast(src):
            return src.partition_broadcast(P)

        with nc.Block() as block:
            @block.sync
            def _(sp):
                blocks = [
                    [(w * 512, W.rearrange("(k p) n -> p k n", p=P)) for w, W in enumerate((Wq, Wk, Wv, Wo))],
                    [(w * 512, W.rearrange("(k p) n -> p k n", p=P)) for w, W in enumerate((L2W, L2attn, L3W))],
                ] + [[(0, W1[l].rearrange("(k p) n -> p k n", p=P))] for l in range(L1N)] \
                  + [[(0, W2[l].rearrange("(k p) n -> p k n", p=P))] for l in range(L1N)]
                for i, parts in enumerate(blocks):
                    if i >= 2:
                        sp.wait_ge(split, 2 * (i - 1))
                    for col, src in parts:
                        k, n = src.shape[1], src.shape[2]
                        sp.dma_start(stage[i % 2][:, col:col + k * n].rearrange("p (k n) -> p k n", k=k), src)\
                          .then_inc(loaded[i], 16)

            @block.scalar
            def _(act):
                def load(dst, src, small=False):
                    act.dma_start(dst, src, allow_slow_non_contiguous=small).then_inc(const_ready, 16)
                load(g1_bc[:, :, :], bcast(g1))
                load(res_bc[:, :, :], bcast(beta1))
                load(g2_bc[:, :, :], bcast(g2))
                load(beta2_bc[:, :, :], bcast(beta2))
                load(arena[:, 0:L1N * D].rearrange("p (l d) -> p l d", l=L1N), bcast(b2))
                load(a_bc[:, 0:L1N, :, :], bcast(attn_w.rearrange("l (a d) -> l a d", a=2)))
                load(a_bc[:, L1N, :, :], bcast(L3a.rearrange("(a d) o -> a (d o)", a=2)))
                load(ab_bc[:, 0:L1N], bcast(attn_b))
                for c in range(ND):
                    load(g1_col[:, :, c], g1[:, c * P:c * P + P].rearrange("l p -> p l"), small=True)
                    load(beta1_col[:, :, c], beta1[:, c * P:c * P + P].rearrange("l p -> p l"), small=True)
                for l in range(L1N):
                    load(b1_col[:, l, :], b1[l].rearrange("(c p) -> p c", p=P), small=True)
                load(l2b_col[:, :], L2b.rearrange("(c p) -> p c", p=P), small=True)
                act.wait_ge(const_ready, 16 * 16)

            @block.gpsimd
            def _(pool):
                nc.gpsimd.memset(ident[:, :], 0.0).then_inc(ident_ready, 1)
                nc.gpsimd.memset(ones[:, :], 1.0).then_inc(ident_ready, 1)
                nc.gpsimd.memset(minus_half[:, :], -0.5).then_inc(ident_ready, 1)
                nc.gpsimd.memset(ab_bc[:, L1N:L1N + 1], 0.0).then_inc(ident_ready, 1)
                pool.wait_ge(ident_ready, 4)
                nc.gpsimd.affine_select(out=ident[:, :], in_=ident[:, :], compare_op=ALU.not_equal, fill=1.0,
                                        base=0, pattern=[[-1, P]], channel_multiplier=1).then_inc(ident_ready, 1)

            @block.tensor
            def _(pe):
                pe.wait_ge(ident_ready, 5)
                pe.wait_ge(loaded[W_TAIL], 16 * 3)
                for i in range(ND):
                    for o in range(ND):
                        last = nc.tensor.transpose(U[0][:, i * D + o * P:i * D + o * P + P],
                                                   stage[1][:, o * D + i * P:o * D + i * P + P], ident[:, :])
                last.then_inc(wT, 1)

            @block.vector
            def _(dve):
                dmas = [4, 3, 1, 1, 1, 1, 1, 1]
                cols = [2048, 1536] + [2048] * 6
                for i in range(NBLK):
                    dve.wait_ge(loaded[i], 16 * dmas[i])
                    src = stage[i % 2][:, 0:cols[i]]
                    first = 0
                    if i == W_TAIL:
                        dve.wait_ge(wT, 1)
                        nc.vector.tensor_copy(WH[:, i, 0:512], U[0][:, :]).then_inc(wT, 1)
                        dve.wait_ge(wT, 2)
                        nc.vector.tensor_tensor(WL[:, i, 0:512], U[0][:, :], WH[:, i, 0:512], ALU.subtract)\
                            .then_inc(wT, 1)
                        first = 512
                    nc.vector.tensor_copy(WH[:, i, first:cols[i]], src[:, first:]).then_inc(split, 1)
                    dve.wait_ge(split, 2 * i + 1)
                    nc.vector.tensor_tensor(WL[:, i, first:cols[i]], src[:, first:], WH[:, i, first:cols[i]],
                                            ALU.subtract).then_inc(split, 1)
                dve.wait_ge(const_ready, 16 * 16)
                nc.vector.tensor_tensor(res_bc[:, :, :], res_bc[:, :, :],
                                        arena[:, 0:L1N * D].rearrange("p (l d) -> p l d", l=L1N),
                                        ALU.add).then_inc(split, 1)
        nc.all_engine_barrier(sems_to_clear=sems)

        class Reader:

            def __init__(self, eng):
                self.eng, self.at = eng, {}

            def wait(self, buf):
                for at in self.at.pop(buf, ()):
                    self.eng.wait_ge(*at)

            def by(self, buf, *ats):
                self.at[buf] = ats

        def wblk(W, blk, w, k, c0, n):
            return W[:, blk, w * 512 + k * D + c0:w * 512 + k * D + c0 + n]

        with nc.Fori(0, B // STREAMS) as it:
            with nc.Block() as block:
                @block.sync
                def _(sp):
                    for s in range(STREAMS):
                        b = it * STREAMS + s
                        sp.dma_start(X[s][:, :, :], x[bass.ds(b, 1), :, :].rearrange("b (p t) d -> p (b t) d", t=NT))\
                          .then_inc(x_in[s], 16)
                        if s:
                            sp.wait_ge(mask_ready[0], 1)
                        sp.dma_start(Z[:, :, :].bitcast(I32),
                                     adj[bass.ds(b, 1), :, :].rearrange("b (p t) j -> p (b t) j", t=NT))\
                          .then_inc(adj_in[s], 16)
                    for s in range(STREAMS):
                        if s:
                            sp.wait_ge(s0_ready[0], NH * NT)
                        for m in range(2):
                            for w, (stack, parts) in enumerate(((QS, (0, 0, 1)), (KS, (0, 1, 0)))):
                                sp.wait_ge(qk_lo[s], 2 * w + m + 1)
                                for g in range(HG):
                                    for i, e in enumerate(parts):
                                        sp.dma_start(stack[DK * i:DK * i + DK, HG * m + g, :],
                                                     ST[DK * g:DK * g + DK, w, m, e, :]).then_inc(stack_in[m][s], 16)
                    for s in range(STREAMS):
                        b = it * STREAMS + s
                        sp.wait_ge(xs_ready[s], 3)
                        sp.dma_start(out[bass.ds(b, 1), :, :].rearrange("b (p t) d -> p (b t) d", t=NT), X[s][:, :, :])\
                          .then_inc(stored[s], 16)
                    for s in range(STREAMS):
                        sp.wait_ge(stored[s], 16)

                @block.gpsimd
                def _(pool):
                    def self_mask(s):
                        pool.wait_ge(mask_ready[s], 2)
                        for t in range(NT):
                            nc.gpsimd.affine_select(out=mask_self[s][:, t, t, :], in_=mask_self[s][:, t, t, :],
                                                    compare_op=ALU.not_equal, fill=0.0, base=0, pattern=[[-1, P]],
                                                    channel_multiplier=1).then_inc(self_ready[s], 1)

                    def norm(s, u):
                        pool.wait_ge(var_ready[s], u + 1)
                        nc.gpsimd.tensor_tensor(rstd[:, :], ve[:, :], minus_half[:, :], ALU.pow)\
                            .then_inc(rstd_ready[s], 1)

                    def residual(s, l):
                        pool.wait_ge(y_ready[s], NT * (2 + 2 * l) + NT)
                        nc.gpsimd.tensor_tensor(RES[s][:, :, :], Y[:, :, :],
                                                g1_bc[:, l:l + 1, :].to_broadcast([P, NT, D]), ALU.mult)\
                            .then_inc(res_half[s], 1)
                        pool.wait_ge(res_half[s], l + 1)
                        nc.gpsimd.tensor_tensor(RES[s][:, :, :], RES[s][:, :, :],
                                                res_bc[:, l:l + 1, :].to_broadcast([P, NT, D]), ALU.add)\
                            .then_inc(res_ready[s], 1)

                    def heads(s):
                        for h in range(NH):
                            pool.wait_ge(r0_ready[s], h + 1)
                            for t in range(NT):
                                nc.gpsimd.tensor_scalar(PR[:, h % 3, t, :], PR[:, h % 3, t, :],
                                                        RINV[:, s, h, t:t + 1], 0.0, ALU.mult, ALU.add)\
                                    .then_inc(pn_ready[s], 1)

                    for s in range(STREAMS):
                        norm(s, 0)
                        if s == 0:
                            self_mask(0)
                            self_mask(1)
                        heads(s)
                    for s in range(STREAMS):
                        norm(s, 1)
                        for l in range(L1N):
                            norm(s, 2 + 2 * l)
                            residual(s, l)
                            norm(s, 3 + 2 * l)
                        norm(s, 8)
                        norm(s, 9)

                @block.tensor
                def _(pe):
                    free = Reader(pe)

                    def mm3(dst, ah, al, bh, bl, start, stop):
                        nc.tensor.matmul(dst, ah, bh, start=start, stop=False, skip_group_check=True)
                        nc.tensor.matmul(dst, ah, bl, start=False, stop=False, skip_group_check=True)
                        return nc.tensor.matmul(dst, al, bh, start=False, stop=stop, skip_group_check=True)

                    def turn(s, u):
                        v = TURN_OF[u]
                        pe.wait_ge(y_ready[s], NT * (u + 1))
                        for c in range(ND):
                            free.wait(f"U{c}")
                            for t in range(NT):
                                last = nc.tensor.transpose(U[c][:, t * P:t * P + P], Y[:, t, c * P:c * P + P], ident[:, :])
                            last.then_inc(yT_ready[s], 1)
                            free.by(f"U{c}", (lo_ready[s], ND * v + c + 1))
                        pe.wait_ge(hi_ready[s], ND * v + ND)
                        pe.wait_ge(lo_ready[s], ND * v + ND)

                    def hT(s, k, c0=0, n=N):
                        return hT_hi[s][:, k, c0:c0 + n], hT_lo[s][:, k, c0:c0 + n]

                    def to_T(bank, s, blk, w, m):
                        for k in range(ND):
                            last = mm3(bank[:, :], wblk(WH, blk, w, k, m * P, P), wblk(WL, blk, w, k, m * P, P),
                                       *hT(s, k), k == 0, k == ND - 1)
                        return last

                    def to_N(banks, s, blk, w):
                        for t in range(NT):
                            for k in range(ND):
                                last = mm3(banks[t // 2][:, (t % 2) * D:(t % 2) * D + D], *hT(s, k, t * P, P),
                                           wblk(WH, blk, w, k, 0, D), wblk(WL, blk, w, k, 0, D),
                                           k == 0 and t % 2 == 0, k == ND - 1)
                            if t % 2:
                                yield last

                    def project(s):
                        for w in range(2):
                            for m in range(2):
                                free.wait(f"U{m}")
                                to_T(U[m], s, W_L0, w, m).then_inc(qk_ps[s], 1)
                                free.by(f"U{m}", (qk_lo[s], 2 * w + m + 1))
                        free.wait("Y0")
                        free.wait("Y1")
                        for i, last in enumerate(to_N(YB, s, W_L0, 2)):
                            last.then_inc(v_ps[s], 1)
                            free.by(f"Y{i}", (v_ready[s], i + 1))

                    def heads(s):
                        def score(h, t):
                            i = h * NT + t
                            free.wait(f"S{t}")
                            nc.tensor.matmul(SB4[t][:, :], QS[0:3 * DK, h, t * P:t * P + P], KS[0:3 * DK, h, :],
                                             start=True, stop=True).then_inc(s0_ready[s], 1)
                            free.by(f"S{t}", (z0_ready[s], i + 1))

                        def turned(h, j):
                            free.wait(f"U{j % 2}")
                            for t in range(NT):
                                last = nc.tensor.transpose(U[j % 2][:, t * P:t * P + P],
                                                           PR[:, h % 3, t, j * P:j * P + P], ident[:, :])
                            last.then_inc(pt0_ps[s], 1)
                            done = pt0_act if j % 2 == 0 else pt0_dve
                            free.by(f"U{j % 2}", (done[s], 2 * h + j // 2 + 1))

                        def weigh(g):
                            free.wait(f"Y{g}")
                            for j in range(NT):
                                for q in range(HG):
                                    h = HG * g + q
                                    last = nc.tensor.matmul(YB[g][DK * q:DK * q + DK, :], V[:, j, DK * h:DK * h + DK],
                                                            PT[:, q, j, :], start=(j == 0), stop=(j == NT - 1))
                            last.then_inc(pv_done[s], 1)
                            free.by(f"Y{g}", (o_lo[s], g + 1))

                        free.wait("stacks")
                        pe.wait_ge(stack_in[0][s], 16 * 24)
                        for t in range(NT):
                            score(0, t)
                        pe.wait_ge(v_ready[s], 2)
                        for i in range(NH + 3):
                            if i == HG + 2 or i == NH + 2:
                                pe.wait_ge(pt0_act[s], 2 * (i - 2))
                                pe.wait_ge(pt0_dve[s], 2 * (i - 2))
                                weigh(i // HG - 1)
                            if 2 <= i < NH + 2:
                                pe.wait_ge(pn_ready[s], NT * (i - 1))
                            for j in range(NT):
                                if 2 <= i < NH + 2:
                                    turned(i - 2, j)
                                if i + 1 < NH:
                                    if i + 1 == HG and j == 0:
                                        pe.wait_ge(stack_in[1][s], 16 * 24)
                                    score(i + 1, j)
                        free.wait("S2")
                        free.wait("S3")
                        pe.wait_ge(o_lo[s], 2)
                        for t in range(NT):
                            for g in range(2):
                                c = slice(t * P, t * P + P)
                                last = mm3(GB[t // 2][:, (t % 2) * D:(t % 2) * D + D], hT_hi[s][:, g, c], hT_lo[s][:, g, c],
                                           wblk(WH, W_L0, 3, g, 0, D), wblk(WL, W_L0, 3, g, 0, D),
                                           g == 0 and t % 2 == 0, g == 1)
                            if t % 2:
                                last.then_inc(wo_done[s], 1)
                                free.by(f"S{2 + t // 2}", (x1_ready[s], t // 2 + 1))

                    def row_scores(s, use):
                        n = use if use < USE_L2 else 3
                        pe.wait_ge(diag_ready[s], NT * (n + 1))
                        free.wait("S0")
                        nc.tensor.matmul(PB[0][:, :], ones[:, :], diag[:, :, :].rearrange("p t n -> p (t n)"),
                                         start=True, stop=True).then_inc(sj_ready[s], 1)
                        free.by("S0", (z_ready[s], NT * (use + 1)))

                    def tail(s, use):
                        pe.wait_ge(p_ready[s], NT * (use + 1))
                        for j in range(NT):
                            free.wait(f"S{j % 2}")
                            for t in range(NT):
                                last = nc.tensor.transpose(PB[j % 2][:, t * P:t * P + P], PR[:, s, t, j * P:j * P + P],
                                                           ident[:, :])
                            last.then_inc(pt_ps[s], 1)
                            free.by(f"S{j % 2}", (pt_lo[s], NT * use + j + 1))
                        pe.wait_ge(pt_lo[s], NT * (use + 1))
                        pe.wait_ge(xlo_ready[s], use + 1)
                        free.wait("S2")
                        free.wait("S3")
                        for t in range(NT):
                            for j in range(NT):
                                c = slice(t * P, t * P + P)
                                last = mm3(GB[t // 2][:, (t % 2) * D:(t % 2) * D + D], PTH[:, j, c], PTL[:, j, c],
                                           XH[s][:, j, :], XL[s][:, j, :], j == 0 and t % 2 == 0, j == NT - 1)
                            if t % 2:
                                last.then_inc(agg_ps[s], 1)
                                used = src_ready if use < USE_L2 else hp_ready
                                n = 4 * use if use < USE_L2 else NT * (use - USE_L2)
                                free.by(f"S{2 + t // 2}", (used[s], (2 * NT * use if use < USE_L2 else n) + t + 1))

                    def forward(s, l):
                        def up(c):
                            free.wait(f"U{c % 2}")
                            for k in range(ND):
                                w = slice(k * HID + c * P, k * HID + c * P + P)
                                last = mm3(U[c % 2][:, :], WH[:, W_UP + l, w], WL[:, W_UP + l, w], *hT(s, k),
                                           k == 0, k == ND - 1)
                            last.then_inc(up_ps[s], 1)
                            free.by(f"U{c % 2}", (g_ready[s], 2 * (NC * l + c + 1)))

                        def down(c):
                            if c == 0:
                                free.wait("Y0")
                                free.wait("Y1")
                            pe.wait_ge(g_ready[s], 2 * (NC * l + c + 1))
                            pe.wait_ge(glo_ready[s], NC * l + c + 1)
                            w = slice(c * D, c * D + D)
                            for t in range(NT):
                                g = slice(t * P, t * P + P)
                                last = mm3(YB[t // 2][:, (t % 2) * D:(t % 2) * D + D], GH[:, c % 2, g], GL[:, c % 2, g],
                                           WH[:, W_DOWN + l, w], WL[:, W_DOWN + l, w], c == 0 and t % 2 == 0, c == NC - 1)
                            last.then_inc(down_done[s], 1)

                        for c in range(NC):
                            up(c)
                            if c:
                                down(c - 1)
                            yield
                        down(NC - 1)
                        n = 2 * NT * l + NT + NT
                        free.by("Y0", (src_ready[s], n))
                        free.by("Y1", (src_ready[s], n))
                        yield

                    def dense(s):
                        for m in range(ND):
                            free.wait(f"U{m}")
                            to_T(U[m], s, W_TAIL, 0, m).then_inc(h2_ps[s], 1)
                            free.by(f"U{m}", (h2_f[s], 2 * (m + 1)))
                        pe.wait_ge(h2_f[s], 2 * ND)
                        for t in range(NT):
                            if t % 2 == 0:
                                free.wait(f"Y{t // 2}")
                            for c in range(ND):
                                last = nc.tensor.transpose(YB[t // 2][:, (t % 2) * D + c * P:(t % 2) * D + c * P + P],
                                                           tT[:, c, t * P:t * P + P], ident[:, :])
                            if t % 2:
                                last.then_inc(hn_ps[s], 1)
                                free.by(f"Y{t // 2}", (xlo_ready[s], USE_L2 + 1))
                        pe.wait_ge(h2_lo[s], ND)
                        for m in range(ND):
                            free.wait(f"U{m}")
                            for k in range(ND):
                                last = mm3(U[m][:, :], wblk(WH, W_TAIL, 1, k, m * P, P), wblk(WL, W_TAIL, 1, k, m * P, P),
                                           *hT(s, k), k == 0, k == ND - 1)
                            last.then_inc(ha_ps[s], 1)
                            free.by(f"U{m}", (ha_lo[s], m + 1))
                        pe.wait_ge(ha_lo[s], ND)
                        for t in range(NT):
                            free.wait(f"S{t}")
                            c = slice(t * P, t * P + P)
                            for k in range(ND):
                                last = mm3(SB4[t][:, :], HAH[:, k, c], HAL[:, k, c], *hT(s, k), k == 0, k == ND - 1)
                            last.then_inc(s2_ps[s], 1)
                            free.by(f"S{t}", (z_ready[s], NT * USE_L2 + t + 1))

                    def wh(s):
                        free.wait("Y0")
                        free.wait("Y1")
                        for i, last in enumerate(to_N(YB, s, W_TAIL, 2)):
                            last.then_inc(hn_ps[s], 1)
                            free.by(f"Y{i}", (xlo_ready[s], USE_L3 + 1))

                    for s in range(STREAMS):
                        turn(s, 0)
                        project(s)
                        heads(s)
                    for s in range(STREAMS):
                        for l in range(L1N):
                            row_scores(s, l)
                            tail(s, l)
                            turn(s, 2 + 2 * l)
                            for _ in forward(s, l):
                                pass
                        turn(s, 8)
                        dense(s)
                        tail(s, USE_L2)
                        turn(s, 9)
                        wh(s)
                        row_scores(s, USE_L3)
                        tail(s, USE_L3)

                @block.scalar
                def _(act):
                    free = Reader(act)

                    def rectified(s, u):
                        v = TURN_OF[u]
                        free.wait(f"hT{s}")
                        for c in range(ND):
                            act.wait_ge(yT_ready[s], ND * v + c + 1)
                            nc.scalar.activation(hT_hi[s][:, c, :], U[c][:, :], ACT.Relu).then_inc(hi_ready[s], 1)

                    def scaled(s, l):
                        v = TURN_OF[2 + 2 * l]
                        free.wait(f"hT{s}")
                        free.wait("tT")
                        for c in range(ND):
                            act.wait_ge(yT_ready[s], ND * v + c + 1)
                            for dst, done in ((tT, t_ready), (hT_hi[s], hi_ready)):
                                nc.scalar.activation(dst[:, c, :], U[c][:, :], ACT.Identity, bias=beta1_col[:, l, c:c + 1],
                                                     scale=g1_col[:, l, c:c + 1]).then_inc(done[s], 1)
                        free.by("tT", (lo_ready[s], ND * v + ND))
                        free.by(f"hT{s}", (down_done[s], NC * (l + 1)))

                    def project(s):
                        for w in range(2):
                            for m in range(2):
                                act.wait_ge(qk_ps[s], 2 * w + m + 1)
                                if s:
                                    act.wait_ge(pv_done[0], 2)
                                nc.scalar.activation(ST[:, w, m, 0, :], U[m][:, :], ACT.Copy).then_inc(qk_hi[s], 1)
                        for i in range(2):
                            act.wait_ge(v_ps[s], i + 1)
                            nc.scalar.activation(V[:, 2 * i:2 * i + 2, :].rearrange("p t d -> p (t d)"), YB[i][:, :],
                                                 ACT.Copy).then_inc(v_ready[s], 1)

                    def heads(s):
                        for i in range(NH + 3):
                            for t in range(NT):
                                if i < NH:
                                    n = i * NT + t
                                    if i >= 3 and t == 0:
                                        act.wait_ge(pt0_ps[s], NT * (i - 2))
                                    elif s and i == 0 and t == 0:
                                        act.wait_ge(pt0_ps[0], NT * NH)
                                    act.wait_ge(z0_ready[s], n + 1)
                                    nc.scalar.activation(PR[:, i % 3, t, :], Z[:, t, :], ACT.Exp, scale=-1.0,
                                                         bias=NMIN[:, s, i, t:t + 1],
                                                         accum_out=RSUM[:, s, i, t:t + 1]).then_inc(p0_ready[s], 1)
                                if 2 <= i < NH + 2 and t % 2 == 0:
                                    h, j = i - 2, t
                                    if h == 0 and t == 0:
                                        for m in range(2):
                                            act.wait_ge(stack_in[m][s], 16 * 24)
                                    if h == HG:
                                        act.wait_ge(pv_done[s], 1)
                                    act.wait_ge(pt0_ps[s], NT * h + j + 1)
                                    nc.scalar.activation(PT[:, h % HG, j, :], U[0][:, :], ACT.Copy).then_inc(pt0_act[s], 1)
                            if i == HG + 2 or i == NH + 2:
                                g = i // HG - 1
                                act.wait_ge(pv_done[s], g + 1)
                                nc.scalar.activation(hT_hi[s][:, g, :], YB[g][:, :], ACT.Relu).then_inc(o_hi[s], 1)
                        free.by(f"hT{s}", (wo_done[s], 2))

                    def rank1(s, use):
                        n = use if use < USE_L2 else 3
                        act.wait_ge(small_ready[s], n + 1)
                        for t in range(NT):
                            act.wait_ge(z_ready[s], NT * use + t + 1)
                            nc.scalar.activation(PR[:, s, t, :], Z[:, t, :], ACT.Relu, scale=1.0 - SLOPE,
                                                 bias=eb[:, s, 0, t:t + 1]).then_inc(relu_ready[s], 1)
                        for t in range(NT):
                            act.wait_ge(w_ready[s], NT * n + t + 1)
                            nc.scalar.activation(PR[:, s, t, :], Z[:, t, :], ACT.Exp, bias=eb[:, s, 1, t:t + 1],
                                                 accum_out=RSUM[:, s, 0, t:t + 1]).then_inc(p_ready[s], 1)

                    def upper(s, use):
                        free.wait("PTH")
                        for j in range(NT):
                            act.wait_ge(pt_ps[s], NT * use + j + 1)
                            nc.scalar.activation(PTH[:, j, :], PB[j % 2][:, :], ACT.Copy).then_inc(pt_hi[s], 1)
                        free.by("PTH", (agg_ps[s], 2 * (use + 1)))

                    def forward(s, l):
                        for c in range(NC):
                            n = NC * l + c
                            act.wait_ge(up_ps[s], n + 1)
                            free.wait(f"GF{c % 2}")
                            for dst in (GF, GH):
                                nc.scalar.activation(dst[:, c % 2, :], U[c % 2][:, :], ACT.Gelu,
                                                     bias=b1_col[:, l, c:c + 1]).then_inc(g_ready[s], 1)
                            free.by(f"GF{c % 2}", (down_done[s], n + 1))
                            yield

                    def dense(s):
                        free.wait("tT")
                        free.wait(f"hT{s}")
                        for m in range(ND):
                            act.wait_ge(h2_ps[s], ND)
                            for dst in (tT, hT_hi[s]):
                                nc.scalar.activation(dst[:, m, :], U[m][:, :], ACT.Identity, bias=l2b_col[:, m:m + 1])\
                                    .then_inc(h2_f[s], 1)
                        for i in range(2):
                            act.wait_ge(hn_ps[s], i + 1)
                            nc.scalar.activation(XH[s][:, 2 * i:2 * i + 2, :].rearrange("p t d -> p (t d)"), YB[i][:, :],
                                                 ACT.Copy).then_inc(xhi_ready[s], 1)
                        for m in range(ND):
                            act.wait_ge(ha_ps[s], m + 1)
                            nc.scalar.activation(HAH[:, m, :], U[m][:, :], ACT.Copy).then_inc(ha_hi[s], 1)
                        for t in range(NT):
                            act.wait_ge(z_ready[s], NT * USE_L2 + t + 1)
                            nc.scalar.activation(PR[:, s, t, :], Z[:, t, :], ACT.Exp, scale=-1.0,
                                                 bias=NMIN[:, s, 0, t:t + 1],
                                                 accum_out=RSUM[:, s, 0, t:t + 1]).then_inc(p_ready[s], 1)
                        free.by("tT", (h2_lo[s], ND))
                        free.by(f"hT{s}", (s2_ps[s], NT))

                    def wh(s):
                        for i in range(2):
                            act.wait_ge(hn_ps[s], 3 + i)
                            for dst, done in ((XN[s], xn_ready), (XH[s], xhi_ready)):
                                nc.scalar.activation(dst[:, 2 * i:2 * i + 2, :].rearrange("p t d -> p (t d)"),
                                                     YB[i][:, :], ACT.Copy).then_inc(done[s], 1)

                    def elu(s, i):
                        act.wait_ge(mn_ready[s], i + 1)
                        nc.scalar.activation(RES[s][:, :, :], RES[s][:, :, :], ACT.Exp).then_inc(ex_ready[s], 1)

                    for s in range(STREAMS):
                        rectified(s, 0)
                        project(s)
                        heads(s)
                    for s in range(STREAMS):
                        for l in range(L1N):
                            rank1(s, l)
                            upper(s, l)
                            scaled(s, l)
                            for _ in forward(s, l):
                                pass
                        rectified(s, 8)
                        free.by(f"hT{s}", (h2_ps[s], ND))
                        dense(s)
                        upper(s, USE_L2)
                        elu(s, 0)
                        rectified(s, 9)
                        free.by(f"hT{s}", (hn_ps[s], 4))
                        wh(s)
                        rank1(s, USE_L3)
                        upper(s, USE_L3)
                        elu(s, 1)

                @block.vector
                def _(dve):
                    free = Reader(dve)
                    v = nc.vector

                    def masks(s):
                        dve.wait_ge(adj_in[s], 16)
                        v.tensor_scalar(mask[s][:, :, :, :],
                                        Z[:, :, :].bitcast(I32).rearrange("p t (q j) -> p t j q", j=NT),
                                        0.0, MASKED, ALU.is_equal, ALU.mult).then_inc(mask_ready[s], 1)
                        dve.wait_ge(mask_ready[s], 1)
                        v.tensor_copy(mask_self[s][:, :, :, :], mask[s][:, :, :, :]).then_inc(mask_ready[s], 1)

                    def norm(s, u, src):
                        for t in range(NT):
                            v.bn_stats(stats[:, t, :], src[:, t, :]).then_inc(stat_done[s], 1)
                        for t in range(NT):
                            dve.wait_ge(stat_done[s], NT * u + t + 1)
                            v.bn_aggr(mv[:, t, :], stats[:, t, :]).then_inc(aggr_done[s], 1)
                        dve.wait_ge(aggr_done[s], NT * (u + 1))
                        v.tensor_scalar(ve[:, :], mv[:, :, 1], EPS, None, ALU.add).then_inc(var_ready[s], 1)
                        dve.wait_ge(rstd_ready[s], u + 1)
                        free.wait("Y")
                        for t in range(NT):
                            v.tensor_scalar(Y[:, t, :], src[:, t, :], mv[:, t, 0:1], rstd[:, t:t + 1],
                                            ALU.subtract, ALU.mult).then_inc(y_ready[s], 1)
                        if u in TURN_OF:
                            n = ND * (TURN_OF[u] + 1)
                            if u in (2, 4, 6):
                                free.by("Y", (yT_ready[s], n), (res_half[s], u // 2))
                            else:
                                free.by("Y", (yT_ready[s], n))

                    def rectified(s, u):
                        n = ND * TURN_OF[u]
                        for c in range(ND):
                            dve.wait_ge(hi_ready[s], n + c + 1)
                            v.scalar_tensor_tensor(hT_lo[s][:, c, :], U[c][:, :], 0.0, hT_hi[s][:, c, :],
                                                   ALU.max, ALU.subtract).then_inc(lo_ready[s], 1)

                    def scaled(s, l):
                        n = ND * TURN_OF[2 + 2 * l]
                        for c in range(ND):
                            dve.wait_ge(hi_ready[s], n + c + 1)
                            dve.wait_ge(t_ready[s], ND * l + c + 1)
                            v.tensor_tensor(hT_lo[s][:, c, :], tT[:, c, :], hT_hi[s][:, c, :], ALU.subtract)\
                                .then_inc(lo_ready[s], 1)

                    def project(s):
                        for w in range(2):
                            for m in range(2):
                                dve.wait_ge(qk_hi[s], 2 * w + m + 1)
                                v.tensor_tensor(ST[:, w, m, 1, :], U[m][:, :], ST[:, w, m, 0, :], ALU.subtract)\
                                    .then_inc(qk_lo[s], 1)

                    def heads(s):
                        for i in range(NH + 3):
                            for t in range(NT):
                                if i < NH:
                                    n = i * NT + t
                                    dve.wait_ge(s0_ready[s], n + 1)
                                    if i:
                                        dve.wait_ge(p0_ready[s], n - NT + 1)
                                    v.tensor_tensor_reduce(
                                        out=Z[:, t, :], in0=SB4[t][:, :],
                                        in1=mask[s][:, t, :, :].rearrange("p j q -> p (j q)"), scale=NEG_SCALE,
                                        scalar=3e38, op0=ALU.add, op1=ALU.min,
                                        accum_out=NMIN[:, s, i, t:t + 1]).then_inc(z0_ready[s], 1)
                                if t == 1 and 1 <= i <= NH:
                                    dve.wait_ge(p0_ready[s], NT * i)
                                    v.reciprocal(RINV[:, s, i - 1, :], RSUM[:, s, i - 1, :]).then_inc(r0_ready[s], 1)
                                if 2 <= i < NH + 2 and t % 2:
                                    h, j = i - 2, t
                                    if h == 0 and t == 1:
                                        for m in range(2):
                                            dve.wait_ge(stack_in[m][s], 16 * 24)
                                    if h == HG:
                                        dve.wait_ge(pv_done[s], 1)
                                    dve.wait_ge(pt0_ps[s], NT * h + j + 1)
                                    v.tensor_copy(PT[:, h % HG, j, :], U[1][:, :]).then_inc(pt0_dve[s], 1)
                            if i == HG + 2 or i == NH + 2:
                                g = i // HG - 1
                                dve.wait_ge(o_hi[s], g + 1)
                                v.scalar_tensor_tensor(hT_lo[s][:, g, :], YB[g][:, :], 0.0, hT_hi[s][:, g, :],
                                                       ALU.max, ALU.subtract).then_inc(o_lo[s], 1)
                        for i in range(2):
                            dve.wait_ge(wo_done[s], i + 1)
                            xs = X[s][:, 2 * i:2 * i + 2, :].rearrange("p t d -> p (t d)")
                            v.tensor_tensor(xs, xs, GB[i][:, :], ALU.add).then_inc(x1_ready[s], 1)

                    def parts(s, use):
                        dve.wait_ge(xn_ready[s], use + 1)
                        if use:
                            dve.wait_ge(agg_ps[s], 2 * use)
                        v.tensor_copy(XH[s][:, :, :], XN[s][:, :, :]).then_inc(xhi_ready[s], 1)
                        dve.wait_ge(xhi_ready[s], use + 1)
                        v.tensor_tensor(XL[s][:, :, :], XN[s][:, :, :], XH[s][:, :, :], ALU.subtract)\
                            .then_inc(xlo_ready[s], 1)

                    def rank1(s, use):
                        n = use if use < USE_L2 else 3
                        si, sj, c, top, u1, u2 = (sml[:, i, :] for i in range(6))
                        free.wait("Z")
                        for t in range(NT):
                            for dst, a in ((sj, 1), (si, 0)):
                                v.tensor_tensor_reduce(out=Z[:, t, a * D:a * D + D], in0=XN[s][:, t, :],
                                                       in1=a_bc[:, n, a, :], scale=1.0, scalar=0.0, op0=ALU.mult,
                                                       op1=ALU.add, accum_out=dst[:, t:t + 1]).then_inc(dot_done[s], 1)
                        for t in range(NT):
                            dve.wait_ge(dot_done[s], 2 * NT * n + 2 * t + 2)
                            v.tensor_scalar(diag[:, t, :], ident[:, :], sj[:, t:t + 1], None, ALU.mult)\
                                .then_inc(diag_ready[s], 1)
                        v.tensor_scalar(c, si, ab_bc[:, n:n + 1], None, ALU.add).then_inc(small_done[s], 1)
                        dve.wait_ge(sj_ready[s], n + 1)
                        m = mask_self if use < USE_L2 else mask
                        if use < USE_L2:
                            dve.wait_ge(self_ready[s], NT)
                        for t in range(NT):
                            v.tensor_tensor_reduce(out=Z[:, t, :], in0=PB[0][:, :],
                                                   in1=m[s][:, t, :, :].rearrange("p j q -> p (j q)"), scale=1.0,
                                                   scalar=-3e38, op0=ALU.add, op1=ALU.max,
                                                   accum_out=top[:, t:t + 1]).then_inc(z_ready[s], 1)
                        k = 5 * n

                        def then(i, last=small_done):
                            i.then_inc(small_done[s], 1)
                        dve.wait_ge(small_done[s], k + 1)
                        then(v.tensor_scalar(eb[:, s, 0, :], c, 1.0 - SLOPE, None, ALU.mult))
                        dve.wait_ge(z_ready[s], NT * (use + 1))
                        then(v.tensor_tensor(u1, top, c, ALU.add))
                        dve.wait_ge(small_done[s], k + 3)
                        then(v.scalar_tensor_tensor(u2, u1, SLOPE, u1, ALU.mult, ALU.max))
                        dve.wait_ge(small_done[s], k + 4)
                        then(v.scalar_tensor_tensor(eb[:, s, 1, :], c, SLOPE, u2, ALU.mult, ALU.subtract))
                        dve.wait_ge(small_done[s], k + 5)
                        v.tensor_copy(sml[:, 7, :], eb[:, s, 1, :]).then_inc(small_ready[s], 1)
                        for t in range(NT):
                            dve.wait_ge(relu_ready[s], NT * n + t + 1)
                            v.scalar_tensor_tensor(Z[:, t, :], Z[:, t, :], SLOPE, PR[:, s, t, :], ALU.mult, ALU.add)\
                                .then_inc(w_ready[s], 1)
                        free.by("Z", (p_ready[s], NT * (use + 1)))

                    def lower(s, use):
                        for j in range(NT):
                            dve.wait_ge(pt_hi[s], NT * use + j + 1)
                            v.tensor_tensor(PTL[:, j, :], PB[j % 2][:, :], PTH[:, j, :], ALU.subtract)\
                                .then_inc(pt_lo[s], 1)
                        dve.wait_ge(p_ready[s], NT * (use + 1))
                        v.reciprocal(RINV[:, s, 0, :], RSUM[:, s, 0, :]).then_inc(rinv_ready[s], 1)
                        dve.wait_ge(rinv_ready[s], use + 1)

                    def aggregated(s, l):
                        for t in range(NT):
                            dve.wait_ge(agg_ps[s], 2 * l + t // 2 + 1)
                            v.scalar_tensor_tensor(XN[s][:, t, :], GB[t // 2][:, (t % 2) * D:(t % 2) * D + D],
                                                   RINV[:, s, 0, t:t + 1], XN[s][:, t, :], ALU.mult, ALU.add)\
                                .then_inc(src_ready[s], 1)
                        dve.wait_ge(src_ready[s], 2 * NT * l + NT)

                    def forward(s, l):
                        for c in range(NC):
                            n = NC * l + c
                            dve.wait_ge(g_ready[s], 2 * n + 2)
                            free.wait(f"GL{c % 2}")
                            v.tensor_tensor(GL[:, c % 2, :], GF[:, c % 2, :], GH[:, c % 2, :], ALU.subtract)\
                                .then_inc(glo_ready[s], 1)
                            free.by(f"GL{c % 2}", (down_done[s], n + 1))
                            yield
                        dve.wait_ge(down_done[s], NC * (l + 1))
                        dve.wait_ge(res_ready[s], l + 1)
                        for t in range(NT):
                            v.tensor_tensor(XN[s][:, t, :], YB[t // 2][:, (t % 2) * D:(t % 2) * D + D], RES[s][:, t, :],
                                            ALU.add).then_inc(src_ready[s], 1)
                        dve.wait_ge(src_ready[s], 2 * NT * l + 2 * NT)
                        yield

                    def next_x(s, l):
                        dve.wait_ge(y_ready[s], NT * (4 + 2 * l))
                        v.tensor_tensor(XN[s][:, :, :], Y[:, :, :], g2_bc[:, l:l + 1, :].to_broadcast([P, NT, D]),
                                        ALU.mult).then_inc(half_done[s], 1)
                        dve.wait_ge(half_done[s], l + 1)
                        v.tensor_tensor(XN[s][:, :, :], XN[s][:, :, :], beta2_bc[:, l:l + 1, :].to_broadcast([P, NT, D]),
                                        ALU.add).then_inc(xn_ready[s], 1)

                    def dense(s):
                        for m in range(ND):
                            dve.wait_ge(h2_f[s], 2 * (m + 1))
                            v.tensor_tensor(hT_lo[s][:, m, :], tT[:, m, :], hT_hi[s][:, m, :], ALU.subtract)\
                                .then_inc(h2_lo[s], 1)
                        for i in range(2):
                            dve.wait_ge(xhi_ready[s], L1N + i + 1)
                            c = slice(2 * i, 2 * i + 2)
                            last = v.tensor_tensor(XL[s][:, c, :].rearrange("p t d -> p (t d)"), YB[i][:, :],
                                                   XH[s][:, c, :].rearrange("p t d -> p (t d)"), ALU.subtract)
                        last.then_inc(xlo_ready[s], 1)
                        for m in range(ND):
                            dve.wait_ge(ha_hi[s], m + 1)
                            v.tensor_tensor(HAL[:, m, :], U[m][:, :], HAH[:, m, :], ALU.subtract).then_inc(ha_lo[s], 1)
                        free.wait("Z")
                        for t in range(NT):
                            dve.wait_ge(s2_ps[s], t + 1)
                            v.tensor_tensor_reduce(out=Z[:, t, :], in0=SB4[t][:, :],
                                                   in1=mask[s][:, t, :, :].rearrange("p j q -> p (j q)"), scale=-1.0,
                                                   scalar=3e38, op0=ALU.add, op1=ALU.min,
                                                   accum_out=NMIN[:, s, 0, t:t + 1]).then_inc(z_ready[s], 1)
                        free.by("Z", (p_ready[s], NT * (USE_L2 + 1)))

                    def wh(s):
                        for i in range(2):
                            dve.wait_ge(xhi_ready[s], L1N + 2 + i + 1)
                            c = slice(2 * i, 2 * i + 2)
                            last = v.tensor_tensor(XL[s][:, c, :].rearrange("p t d -> p (t d)"), YB[i][:, :],
                                                   XH[s][:, c, :].rearrange("p t d -> p (t d)"), ALU.subtract)
                        last.then_inc(xlo_ready[s], 1)
                        dve.wait_ge(xn_ready[s], L1N + 1 + 2)

                    def elu(s, i):
                        for t in range(NT):
                            dve.wait_ge(agg_ps[s], 2 * (USE_L2 + i) + t // 2 + 1)
                            v.tensor_scalar(XN[s][:, t, :], GB[t // 2][:, (t % 2) * D:(t % 2) * D + D],
                                            RINV[:, s, 0, t:t + 1], None, ALU.mult).then_inc(hp_ready[s], 1)
                        dve.wait_ge(hp_ready[s], NT * (i + 1))
                        v.tensor_scalar(RES[s][:, :, :], XN[s][:, :, :], 0.0, None, ALU.min).then_inc(mn_ready[s], 1)
                        dve.wait_ge(ex_ready[s], i + 1)
                        v.scalar_tensor_tensor(XN[s][:, :, :], XN[s][:, :, :], 0.0, RES[s][:, :, :], ALU.max, ALU.add)\
                            .then_inc(el_ready[s], 1)
                        dve.wait_ge(el_ready[s], i + 1)
                        v.scalar_tensor_tensor(X[s][:, :, :], XN[s][:, :, :], -1.0, X[s][:, :, :], ALU.add, ALU.add)\
                            .then_inc(xs_ready[s], 1)
                        dve.wait_ge(xs_ready[s], i + 2)

                    for s in range(STREAMS):
                        if s == 0:
                            masks(0)
                        dve.wait_ge(x_in[s], 16)
                        norm(s, 0, X[s])
                        rectified(s, 0)
                        if s == 0:
                            masks(1)
                        project(s)
                        heads(s)
                    for s in range(STREAMS):
                        dve.wait_ge(x1_ready[s], 2)
                        norm(s, 1, X[s])
                        dve.wait_ge(y_ready[s], NT * 2)
                        v.tensor_scalar(XN[s][:, :, :], Y[:, :, :], 0.0, None, ALU.max).then_inc(xn_ready[s], 1)
                        for l in range(L1N):
                            parts(s, l)
                            rank1(s, l)
                            lower(s, l)
                            aggregated(s, l)
                            norm(s, 2 + 2 * l, XN[s])
                            scaled(s, l)
                            for _ in forward(s, l):
                                pass
                            norm(s, 3 + 2 * l, XN[s])
                            next_x(s, l)
                        dve.wait_ge(xn_ready[s], L1N + 1)
                        v.tensor_tensor(X[s][:, :, :], X[s][:, :, :], XN[s][:, :, :], ALU.add).then_inc(xs_ready[s], 1)
                        dve.wait_ge(xs_ready[s], 1)
                        norm(s, 8, X[s])
                        rectified(s, 8)
                        dense(s)
                        lower(s, USE_L2)
                        elu(s, 0)
                        norm(s, 9, X[s])
                        rectified(s, 9)
                        wh(s)
                        rank1(s, USE_L3)
                        lower(s, USE_L3)
                        elu(s, 1)
            nc.all_engine_barrier(sems_to_clear=sems)


_INS = ["x", "adj", "L0_gnn_Wq", "L0_gnn_Wk", "L0_gnn_Wv", "L0_gnn_Wo", "L1_gnn_attn_w", "L1_gnn_attn_b",
        "L1_gnn_W1", "L1_gnn_b1", "L1_gnn_W2", "L1_gnn_b2", "L1_gnn_g1", "L1_gnn_beta1", "L1_gnn_g2",
        "L1_gnn_beta2", "L2_gnn_W", "L2_gnn_b", "L2_gnn_attn", "L3_gnn_W", "L3_gnn_a"]


def kernel(**inputs):
    import numpy as np
    import concourse.bacc as bacc
    from concourse.bass_utils import run_bass_kernel_spmd

    nc = bacc.Bacc("TRN2", target_bir_lowering=False, num_devices=1)
    arrays, args = {}, []
    for name in _INS:
        a = np.ascontiguousarray(inputs[name])
        arrays[f"in_{name}"] = a
        args.append(nc.dram_tensor(f"in_{name}", a.shape, mybir.dt.from_np(a.dtype), kind="ExternalInput").ap())
    args.append(nc.dram_tensor("out", (B, N, D), F32, kind="ExternalOutput").ap())
    build(nc, *args)
    r = run_bass_kernel_spmd(nc, [arrays], core_ids=[0])
    return r.results[0]["out"]
```

```python
from contextlib import ExitStack

import concourse.bass as bass
from concourse import mybir

F32 = mybir.dt.float32
F16 = mybir.dt.float16
BF16 = mybir.dt.bfloat16
I32 = mybir.dt.int32
ALU = mybir.AluOpType
ACT = mybir.ActivationFunctionType

P = 128
B, N, D = 16, 512, 256
NT = N // P
ND = D // P
NH, DK = 8, 32
HG = P // DK
L1N = 3
HID = 4 * D
NC = HID // P
EPS = 1e-5
MASKED = -1e30
NEG_SCALE = -float(DK) ** -0.5
SLOPE = 0.2
STREAMS = 2
LAG = 27.0

W_L0, W_TAIL, W_UP, W_DOWN = 0, 1, 2, 5
NBLK = 8
USE_L2, USE_L3 = 3, 4
TURN_OF = {0: 0, 2: 1, 4: 2, 6: 3, 8: 4, 9: 5}


def build(nc, x, adj, Wq, Wk, Wv, Wo, attn_w, attn_b, W1, b1, W2, b2, g1, beta1, g2, beta2,
          L2W, L2b, L2attn, L3W, L3a, out):
    ctx = ExitStack()
    with ctx:
        def sb(name, shape, dt):
            return ctx.enter_context(nc.sbuf_tensor(name, shape, dt))

        WH = sb("weights_hi", [P, NBLK, 2048], F16)
        WL = sb("weights_lo", [P, NBLK, 2048], F16)
        ident = sb("ident", [P, P], F32)
        ones = sb("ones", [P, P], F32)
        minus_half = sb("minus_half", [P, NT], F32)
        g1_bc = sb("g1_bc", [P, L1N, D], F32)
        res_bc = sb("beta1_b2_bc", [P, L1N, D], F32)
        g2_bc = sb("g2_bc", [P, L1N, D], F32)
        beta2_bc = sb("beta2_bc", [P, L1N, D], F32)
        a_bc = sb("a_bc", [P, L1N + 1, 2, D], F32)
        ab_bc = sb("attn_b_bc", [P, L1N + 1], F32)
        g1_col = sb("g1_col", [P, L1N, ND], F32)
        beta1_col = sb("beta1_col", [P, L1N, ND], F32)
        b1_col = sb("b1_col", [P, L1N, NC], F32)
        l2b_col = sb("l2b_col", [P, ND], F32)
        X = [sb(f"x{s}", [P, NT, D], F32) for s in range(2)]
        mask = [sb(f"mask{s}", [P, NT, NT, P], BF16) for s in range(2)]
        mask_self = [sb(f"mask_self{s}", [P, NT, NT, P], BF16) for s in range(2)]
        Y = sb("y", [P, NT, D], F32)
        hT_hi = [sb(f"hT_hi{s}", [P, ND, N], F16) for s in range(2)]
        hT_lo = [sb(f"hT_lo{s}", [P, ND, N], F16) for s in range(2)]
        tT = sb("tT", [P, ND, N], F32)
        Z = sb("z", [P, NT, N], F32)
        PR = sb("probs", [P, 3, NT, N], F32)
        V = tT[:, :, :].rearrange("p c (a d) -> p (c a) d", a=2)
        arena = sb("arena", [P, 12288], F32)
        PT = arena[:, 0:8192].rearrange("p (h j n) -> p h j n", h=HG, j=NT)
        ST = arena[:, 0:2048].bitcast(F16).rearrange("p (w m e n) -> p w m e n", w=2, m=2, e=2)
        QS = arena[:, 8192:10240].bitcast(F16).rearrange("p (h n) -> p h n", h=NH)
        KS = arena[:, 10240:12288].bitcast(F16).rearrange("p (h n) -> p h n", h=NH)
        XN = [arena[:, 1024 * s:1024 * s + 1024].rearrange("p (t d) -> p t d", t=NT) for s in range(2)]
        RES = [arena[:, 2048 + 1024 * s:3072 + 1024 * s].rearrange("p (t d) -> p t d", t=NT) for s in range(2)]
        XH = [arena[:, 4096 + 1024 * s:4608 + 1024 * s].bitcast(F16).rearrange("p (t d) -> p t d", t=NT) for s in range(2)]
        XL = [arena[:, 4608 + 1024 * s:5120 + 1024 * s].bitcast(F16).rearrange("p (t d) -> p t d", t=NT) for s in range(2)]
        PTH = arena[:, 6144:7168].bitcast(F16).rearrange("p (j n) -> p j n", j=NT)
        PTL = arena[:, 7168:8192].bitcast(F16).rearrange("p (j n) -> p j n", j=NT)
        GF = arena[:, 8192:9216].rearrange("p (r n) -> p r n", r=2)
        GH = arena[:, 9216:9728].bitcast(F16).rearrange("p (r n) -> p r n", r=2)
        GL = arena[:, 9728:10240].bitcast(F16).rearrange("p (r n) -> p r n", r=2)
        HAH = arena[:, 10240:10752].bitcast(F16).rearrange("p (m n) -> p m n", m=ND)
        HAL = arena[:, 10752:11264].bitcast(F16).rearrange("p (m n) -> p m n", m=ND)
        diag = arena[:, 11264:11776].rearrange("p (t n) -> p t n", t=NT)
        ZS = [Z, PR[:, 2, :, :]]
        NMIN = sb("nmin", [P, 2, NH, NT], F32)
        RSUM = sb("rsum", [P, 2, NH, NT], F32)
        RINV = sb("rinv", [P, 2, NH, NT], F32)
        stats = sb("stats", [P, 2, NT, 6], F32)
        mv = sb("mv", [P, 2, NT, 2], F32)
        ve = sb("ve", [P, 2, NT], F32)
        rstd = sb("rstd", [P, 2, NT], F32)
        sml = sb("small", [P, 2, 8, NT], F32)
        eb = sb("eb", [P, 2, 2, NT], F32)
        U = [ctx.enter_context(nc.psum_tensor(f"U{i}", [P, 512], F32)) for i in range(2)]
        YB = [ctx.enter_context(nc.psum_tensor(f"Y{i}", [P, 512], F32)) for i in range(2)]
        PB = [ctx.enter_context(nc.psum_tensor(f"P{i}", [P, 512], F32)) for i in range(2)]
        GB = [ctx.enter_context(nc.psum_tensor(f"G{i}", [P, 512], F32)) for i in range(2)]
        SB4, SCORE = [PB[0], PB[1], GB[0], GB[1]], ["P0", "P1", "G0", "G1"]

        def sem(name):
            return ctx.enter_context(nc.semaphore(name))

        def per_stream(name):
            return [sem(f"{name}{s}") for s in range(STREAMS)]

        loaded = [sem(f"loaded{i}") for i in range(NBLK)]
        split, wT = sem("split"), sem("wT")
        const_ready, ident_ready = sem("const_ready"), sem("ident_ready")
        x_in, adj_in = per_stream("x_in"), per_stream("adj_in")
        mask_ready, self_ready = per_stream("mask_ready"), per_stream("self_ready")
        stat_done, var_ready, rstd_ready = (per_stream(n) for n in ("stat", "var", "rstd"))
        y_ready, yT_ready, hi_ready, lo_ready, t_ready = (per_stream(n) for n in ("y", "yT", "hT_hi", "hT_lo", "tT"))
        qk_ps, qk_hi, qk_lo = per_stream("qk_ps"), per_stream("qk_hi"), per_stream("qk_lo")
        stack_in = [[sem(f"stack{m}_{s}") for s in range(2)] for m in range(2)]
        v_ps, v_ready = per_stream("v_ps"), per_stream("v_sb")
        s0_ready, z0_ready, p0_ready, r0_ready, pn_ready, pt0_ps, pt0_act, pt0_dve, pv_done = (
            per_stream(n) for n in ("s0", "z0", "p0", "r0", "pn", "pt0", "pt0_act", "pt0_dve", "pv"))
        o_hi, o_lo, wo_done, x1_ready = (per_stream(n) for n in ("o_hi", "o_lo", "wo", "x1"))
        dot_done, diag_ready, sj_ready, z_ready, small_done, small_ready = (
            per_stream(n) for n in ("dot", "diag", "sj", "z", "small", "bias"))
        relu_ready, w_ready, p_ready, pt_ps, pt_hi, pt_lo, agg_ps, rinv_ready = (
            per_stream(n) for n in ("relu", "w", "p", "pt", "pt_hi", "pt_lo", "agg", "rinv"))
        xn_ready, xhi_ready, xlo_ready, src_ready, res_ready = (
            per_stream(n) for n in ("xn", "x_hi", "x_lo", "src", "res"))
        up_ps, g_ready, glo_ready, down_done = (per_stream(n) for n in ("up", "g", "g_lo", "down"))
        h2_ps, h2_f, h2_lo, ha_ps, ha_hi, ha_lo, hn_ps, s2_ps = (
            per_stream(n) for n in ("h2_ps", "h2_f", "h2_lo", "ha_ps", "ha_hi", "ha_lo", "hn_ps", "s2"))
        hp_ready, mn_ready, ex_ready, el_ready, xs_ready = (per_stream(n) for n in ("hp", "mn", "ex", "el", "xs"))
        half_done = per_stream("x_half")
        bounced = per_stream("bounced")
        stored = per_stream("stored")
        sems = range(loaded[0].num, stored[-1].num + 1)

        adj_stage = [Z[:, :, :], PR[:, 0, :, :]]
        bounce = nc.dram_tensor("qk_parts", (STREAMS, 2, 2, P, 2, N), F16).ap()

        stage = [Z[:, :, :].rearrange("p t n -> p (t n)"), PR[:, 0, :, :].rearrange("p t n -> p (t n)")]

        def bcast(src):
            return src.partition_broadcast(P)

        with nc.Block() as block:
            @block.sync
            def _(sp):
                blocks = [
                    [(w * 512, W.rearrange("(k p) n -> p k n", p=P)) for w, W in enumerate((Wq, Wk, Wv, Wo))],
                    [(w * 512, W.rearrange("(k p) n -> p k n", p=P)) for w, W in enumerate((L2W, L2attn, L3W))],
                ] + [[(0, W1[l].rearrange("(k p) n -> p k n", p=P))] for l in range(L1N)] \
                  + [[(0, W2[l].rearrange("(k p) n -> p k n", p=P))] for l in range(L1N)]
                for i, parts in enumerate(blocks):
                    if i >= 2:
                        sp.wait_ge(split, 2 * (i - 1))
                    for col, src in parts:
                        k, n = src.shape[1], src.shape[2]
                        sp.dma_start(stage[i % 2][:, col:col + k * n].rearrange("p (k n) -> p k n", k=k), src)\
                          .then_inc(loaded[i], 16)

            @block.scalar
            def _(act):
                def load(dst, src, small=False):
                    act.dma_start(dst, src, allow_slow_non_contiguous=small).then_inc(const_ready, 16)
                load(g1_bc[:, :, :], bcast(g1))
                load(res_bc[:, :, :], bcast(beta1))
                load(g2_bc[:, :, :], bcast(g2))
                load(beta2_bc[:, :, :], bcast(beta2))
                load(arena[:, 0:L1N * D].rearrange("p (l d) -> p l d", l=L1N), bcast(b2))
                load(a_bc[:, 0:L1N, :, :], bcast(attn_w.rearrange("l (a d) -> l a d", a=2)))
                load(a_bc[:, L1N, :, :], bcast(L3a.rearrange("(a d) o -> a (d o)", a=2)))
                load(ab_bc[:, 0:L1N], bcast(attn_b))
                for c in range(ND):
                    load(g1_col[:, :, c], g1[:, c * P:c * P + P].rearrange("l p -> p l"), small=True)
                    load(beta1_col[:, :, c], beta1[:, c * P:c * P + P].rearrange("l p -> p l"), small=True)
                for l in range(L1N):
                    load(b1_col[:, l, :], b1[l].rearrange("(c p) -> p c", p=P), small=True)
                load(l2b_col[:, :], L2b.rearrange("(c p) -> p c", p=P), small=True)
                act.wait_ge(const_ready, 16 * 16)

            @block.gpsimd
            def _(pool):
                nc.gpsimd.memset(ident[:, :], 0.0).then_inc(ident_ready, 1)
                nc.gpsimd.memset(ones[:, :], 1.0).then_inc(ident_ready, 1)
                nc.gpsimd.memset(minus_half[:, :], -0.5).then_inc(ident_ready, 1)
                nc.gpsimd.memset(ab_bc[:, L1N:L1N + 1], 0.0).then_inc(ident_ready, 1)
                pool.wait_ge(ident_ready, 4)
                nc.gpsimd.affine_select(out=ident[:, :], in_=ident[:, :], compare_op=ALU.not_equal, fill=1.0,
                                        base=0, pattern=[[-1, P]], channel_multiplier=1).then_inc(ident_ready, 1)

            @block.tensor
            def _(pe):
                pe.wait_ge(ident_ready, 5)
                pe.wait_ge(loaded[W_TAIL], 16 * 3)
                for i in range(ND):
                    for o in range(ND):
                        last = nc.tensor.transpose(U[0][:, i * D + o * P:i * D + o * P + P],
                                                   stage[1][:, o * D + i * P:o * D + i * P + P], ident[:, :])
                last.then_inc(wT, 1)

            @block.vector
            def _(dve):
                dmas = [4, 3, 1, 1, 1, 1, 1, 1]
                cols = [2048, 1536] + [2048] * 6
                for i in range(NBLK):
                    dve.wait_ge(loaded[i], 16 * dmas[i])
                    src = stage[i % 2][:, 0:cols[i]]
                    first = 0
                    if i == W_TAIL:
                        dve.wait_ge(wT, 1)
                        nc.vector.tensor_copy(WH[:, i, 0:512], U[0][:, :]).then_inc(wT, 1)
                        dve.wait_ge(wT, 2)
                        nc.vector.tensor_tensor(WL[:, i, 0:512], U[0][:, :], WH[:, i, 0:512], ALU.subtract)\
                            .then_inc(wT, 1)
                        first = 512
                    nc.vector.tensor_copy(WH[:, i, first:cols[i]], src[:, first:]).then_inc(split, 1)
                    dve.wait_ge(split, 2 * i + 1)
                    nc.vector.tensor_tensor(WL[:, i, first:cols[i]], src[:, first:], WH[:, i, first:cols[i]],
                                            ALU.subtract).then_inc(split, 1)
                dve.wait_ge(const_ready, 16 * 16)
                nc.vector.tensor_tensor(res_bc[:, :, :], res_bc[:, :, :],
                                        arena[:, 0:L1N * D].rearrange("p (l d) -> p l d", l=L1N),
                                        ALU.add).then_inc(split, 1)
        nc.all_engine_barrier(sems_to_clear=sems)

        class Reader:

            def __init__(self, eng):
                self.eng, self.at = eng, {}

            def wait(self, buf):
                for at in self.at.pop(buf, ()):
                    self.eng.wait_ge(*at)

            def by(self, buf, *ats):
                self.at[buf] = ats

        rank1_steps = [1.4, 2.5, 1.3, 1.8, 1.3, 1.3]
        tail_steps = [1.0, 1.0, 1.0, 1.0, 0.7, 2.6, 2.6]
        norm_steps = [2.5, 1.0]
        turn_steps = [1.0, 1.2]
        forward_steps = [2.6] * NC + [1.3, 1.3, 3.5, 3.2]
        dense_steps = [2.6, 1.4, 2.6, 2.6, 2.6, 1.3]
        elu_steps = [1.5, 2.2]
        thread = norm_steps + L1N * (rank1_steps + tail_steps + norm_steps + turn_steps + forward_steps) \
            + norm_steps + turn_steps + dense_steps + tail_steps + elu_steps \
            + norm_steps + turn_steps + [2.6] + rank1_steps + tail_steps + elu_steps
        marks = [0] * 2 + L1N * ([0] * 6 + [1] + [2] * 6 + [0] * (4 + len(forward_steps))) \
            + [0] * (4 + len(dense_steps)) + [1] + [2] * 6 + [0] * 2 + [0] * 5 + [0] * 6 + [1] + [2] * 6 + [0] * 2
        assert len(marks) == len(thread)
        plan, done = [], [0, 0]
        while min(done) < len(thread):
            s = min(range(STREAMS), key=lambda s: (done[s] == len(thread), sum(thread[:done[s]]) + s * LAG))
            if done[s] < len(thread) and marks[done[s]] == 1 and marks[min(done[1 - s], len(thread) - 1)] == 2:
                s = 1 - s
            plan.append(s)
            done[s] += 1

        def weave(later):
            threads = [later(s) for s in range(STREAMS)]
            for s in plan:
                next(threads[s])
            assert all(next(t, None) is None for t in threads)

        def wblk(W, blk, w, k, c0, n):
            return W[:, blk, w * 512 + k * D + c0:w * 512 + k * D + c0 + n]

        with nc.Fori(0, B // STREAMS) as it:
            with nc.Block() as block:
                @block.sync
                def _(sp):
                    for s in range(STREAMS):
                        b = it * STREAMS + s
                        sp.dma_start(X[s][:, :, :], x[bass.ds(b, 1), :, :].rearrange("b (p t) d -> p (b t) d", t=NT))\
                          .then_inc(x_in[s], 16)
                        sp.dma_start(adj_stage[s].bitcast(I32),
                                     adj[bass.ds(b, 1), :, :].rearrange("b (p t) j -> p (b t) j", t=NT))\
                          .then_inc(adj_in[s], 16)
                    for s in range(STREAMS):
                        if s:
                            sp.wait_ge(s0_ready[0], NH * NT)
                        for m in range(2):
                            for w in range(2):
                                sp.wait_ge(qk_lo[s], 2 * m + w + 1)
                                sp.dma_start(bounce[s, m, w], ST[:, w, m, :, :]).then_inc(bounced[s], 16)
                            for w, (stack, parts) in enumerate(((QS, (0, 0, 1)), (KS, (0, 1, 0)))):
                                if w == 0:
                                    sp.wait_ge(bounced[s], 32 * (m + 1))
                                for i, e in enumerate(parts):
                                    sp.dma_start(stack[DK * i:DK * i + DK, HG * m:HG * m + HG, :],
                                                 bounce[s, m, w, :, e, :].rearrange("(g r) n -> r g n", g=HG))\
                                      .then_inc(stack_in[m][s], 16)
                    for s in range(STREAMS):
                        b = it * STREAMS + s
                        sp.wait_ge(xs_ready[s], 3)
                        sp.dma_start(out[bass.ds(b, 1), :, :].rearrange("b (p t) d -> p (b t) d", t=NT), X[s][:, :, :])\
                          .then_inc(stored[s], 16)
                    for s in range(STREAMS):
                        sp.wait_ge(stored[s], 16)

                @block.gpsimd
                def _(pool):
                    def self_mask(s):
                        pool.wait_ge(mask_ready[s], 2)
                        for t in range(NT):
                            nc.gpsimd.affine_select(out=mask_self[s][:, t, t, :], in_=mask_self[s][:, t, t, :],
                                                    compare_op=ALU.not_equal, fill=0.0, base=0, pattern=[[-1, P]],
                                                    channel_multiplier=1).then_inc(self_ready[s], 1)

                    def norm(s, u):
                        pool.wait_ge(var_ready[s], u + 1)
                        nc.gpsimd.tensor_tensor(rstd[:, s, :], ve[:, s, :], minus_half[:, :], ALU.pow)\
                            .then_inc(rstd_ready[s], 1)

                    def residual(s, l):
                        pool.wait_ge(y_ready[s], NT * (2 + 2 * l) + NT)
                        nc.gpsimd.tensor_tensor(RES[s][:, :, :], Y[:, :, :],
                                                g1_bc[:, l:l + 1, :].to_broadcast([P, NT, D]), ALU.mult)\
                            .then_inc(res_ready[s], 1)
                        pool.wait_ge(res_ready[s], 2 * l + 1)
                        nc.gpsimd.tensor_tensor(RES[s][:, :, :], RES[s][:, :, :],
                                                res_bc[:, l:l + 1, :].to_broadcast([P, NT, D]), ALU.add)\
                            .then_inc(res_ready[s], 1)

                    def heads(s):
                        for h in range(NH):
                            pool.wait_ge(r0_ready[s], h + 1)
                            for t in range(NT):
                                nc.gpsimd.tensor_scalar(PR[:, h % 3, t, :], PR[:, h % 3, t, :],
                                                        RINV[:, s, h, t:t + 1], 0.0, ALU.mult, ALU.add)\
                                    .then_inc(pn_ready[s], 1)

                    norm(0, 0)
                    norm(1, 0)
                    self_mask(0)
                    self_mask(1)
                    heads(0)
                    heads(1)
                    def lower_x(s, n):
                        pool.wait_ge(xhi_ready[s], n + 1)
                        nc.gpsimd.tensor_tensor(XL[s][:, :, :], XN[s][:, :, :], XH[s][:, :, :], ALU.subtract)\
                            .then_inc(xlo_ready[s], 1)

                    def idle(n):
                        for _ in range(n):
                            yield

                    def later(s):
                        norm(s, 1)
                        yield from idle(2)
                        for l in range(L1N):
                            lower_x(s, l)
                            yield from idle(len(rank1_steps) + len(tail_steps))
                            norm(s, 2 + 2 * l)
                            yield
                            residual(s, l)
                            yield from idle(1 + len(turn_steps) + NC + 2)
                            norm(s, 3 + 2 * l)
                            yield from idle(2)
                        norm(s, 8)
                        yield from idle(2 + len(turn_steps) + len(dense_steps) + len(tail_steps) + len(elu_steps))
                        norm(s, 9)
                        yield from idle(2 + len(turn_steps) + 1 + len(rank1_steps) + len(tail_steps) + len(elu_steps))

                    weave(later)

                @block.tensor
                def _(pe):
                    free = Reader(pe)

                    def mm3(dst, ah, al, bh, bl, start, stop):
                        nc.tensor.matmul(dst, ah, bh, start=start, stop=False, skip_group_check=True)
                        nc.tensor.matmul(dst, ah, bl, start=False, stop=False, skip_group_check=True)
                        return nc.tensor.matmul(dst, al, bh, start=False, stop=stop, skip_group_check=True)

                    def turn(s, u):
                        v = TURN_OF[u]
                        pe.wait_ge(y_ready[s], NT * (u + 1))
                        for c in range(ND):
                            free.wait(f"U{c}")
                            for t in range(NT):
                                last = nc.tensor.transpose(U[c][:, t * P:t * P + P], Y[:, t, c * P:c * P + P], ident[:, :])
                            last.then_inc(yT_ready[s], 1)
                            free.by(f"U{c}", (lo_ready[s], ND * v + c + 1))

                    def h_ready(s, u):
                        pe.wait_ge(hi_ready[s], ND * (TURN_OF[u] + 1))
                        pe.wait_ge(lo_ready[s], ND * (TURN_OF[u] + 1))

                    def hT(s, k, c0=0, n=N):
                        return hT_hi[s][:, k, c0:c0 + n], hT_lo[s][:, k, c0:c0 + n]

                    def to_T(bank, s, blk, w, m):
                        for k in range(ND):
                            last = mm3(bank[:, :], wblk(WH, blk, w, k, m * P, P), wblk(WL, blk, w, k, m * P, P),
                                       *hT(s, k), k == 0, k == ND - 1)
                        return last

                    def to_N(banks, name, s, blk, w):
                        for t in range(NT):
                            if t % 2 == 0:
                                free.wait(f"{name}{t // 2}")
                            for k in range(ND):
                                last = mm3(banks[t // 2][:, (t % 2) * D:(t % 2) * D + D], *hT(s, k, t * P, P),
                                           wblk(WH, blk, w, k, 0, D), wblk(WL, blk, w, k, 0, D),
                                           k == 0 and t % 2 == 0, k == ND - 1)
                            if t % 2:
                                yield last

                    def project(s):
                        h_ready(s, 0)
                        for m in range(2):
                            for w in range(2):
                                free.wait(f"U{w}")
                                to_T(U[w], s, W_L0, w, m).then_inc(qk_ps[s], 1)
                                free.by(f"U{w}", (qk_lo[s], 2 * m + w + 1))
                        for i, last in enumerate(to_N(YB, "Y", s, W_L0, 2)):
                            last.then_inc(v_ps[s], 1)
                            free.by(f"Y{i}", (v_ready[s], i + 1))

                    def heads(s):
                        def score(h, t):
                            i = h * NT + t
                            free.wait(SCORE[t])
                            nc.tensor.matmul(SB4[t][:, :], QS[0:3 * DK, h, t * P:t * P + P], KS[0:3 * DK, h, :],
                                             start=True, stop=True).then_inc(s0_ready[s], 1)
                            free.by(SCORE[t], (z0_ready[s], i + 1))

                        def turned(h, j):
                            free.wait(f"U{j % 2}")
                            for t in range(NT):
                                last = nc.tensor.transpose(U[j % 2][:, t * P:t * P + P],
                                                           PR[:, h % 3, t, j * P:j * P + P], ident[:, :])
                            last.then_inc(pt0_ps[s], 1)
                            done = pt0_act if j % 2 == 0 else pt0_dve
                            free.by(f"U{j % 2}", (done[s], 2 * h + j // 2 + 1))

                        def weigh(g):
                            free.wait(f"Y{g}")
                            for j in range(NT):
                                for q in range(HG):
                                    h = HG * g + q
                                    last = nc.tensor.matmul(YB[g][DK * q:DK * q + DK, :], V[:, j, DK * h:DK * h + DK],
                                                            PT[:, q, j, :], start=(j == 0), stop=(j == NT - 1))
                            last.then_inc(pv_done[s], 1)
                            free.by(f"Y{g}", (o_lo[s], g + 1))

                        free.wait("stacks")
                        pe.wait_ge(stack_in[0][s], 16 * 6)
                        for t in range(NT):
                            score(0, t)
                        pe.wait_ge(v_ready[s], 2)
                        for i in range(NH + 3):
                            if i == HG + 2 or i == NH + 2:
                                pe.wait_ge(pt0_act[s], 2 * (i - 2))
                                pe.wait_ge(pt0_dve[s], 2 * (i - 2))
                                weigh(i // HG - 1)
                            if 2 <= i < NH + 2:
                                pe.wait_ge(pn_ready[s], NT * (i - 1))
                            for j in range(NT):
                                if 2 <= i < NH + 2:
                                    turned(i - 2, j)
                                if i + 1 < NH:
                                    if i + 1 == HG and j == 0:
                                        pe.wait_ge(stack_in[1][s], 16 * 6)
                                    score(i + 1, j)
                        free.wait("G0")
                        free.wait("G1")
                        pe.wait_ge(o_lo[s], 2)
                        for t in range(NT):
                            for g in range(2):
                                c = slice(t * P, t * P + P)
                                last = mm3(GB[t // 2][:, (t % 2) * D:(t % 2) * D + D], hT_hi[s][:, g, c], hT_lo[s][:, g, c],
                                           wblk(WH, W_L0, 3, g, 0, D), wblk(WL, W_L0, 3, g, 0, D),
                                           g == 0 and t % 2 == 0, g == 1)
                            if t % 2:
                                last.then_inc(wo_done[s], 1)
                                free.by(f"G{t // 2}", (x1_ready[s], t // 2 + 1))

                    def row_scores(s, use):
                        n = use if use < USE_L2 else 3
                        pe.wait_ge(diag_ready[s], NT * (n + 1))
                        free.wait("P0")
                        nc.tensor.matmul(PB[0][:, :], ones[:, :], diag[:, :, :].rearrange("p t n -> p (t n)"),
                                         start=True, stop=True).then_inc(sj_ready[s], 1)
                        free.by("P0", (z_ready[s], NT * (use + 1)))

                    def tail(s, use):
                        pe.wait_ge(p_ready[s], NT * (use + 1))
                        for j in range(NT):
                            free.wait(f"P{j % 2}")
                            for t in range(NT):
                                last = nc.tensor.transpose(PB[j % 2][:, t * P:t * P + P], PR[:, s, t, j * P:j * P + P],
                                                           ident[:, :])
                            last.then_inc(pt_ps[s], 1)
                            free.by(f"P{j % 2}", (pt_lo[s], NT * use + j + 1))
                            yield
                        yield
                        pe.wait_ge(pt_lo[s], NT * (use + 1))
                        pe.wait_ge(xlo_ready[s], use + 1)
                        for t in range(NT):
                            if t % 2 == 0:
                                free.wait(f"G{t // 2}")
                            for j in range(NT):
                                c = slice(t * P, t * P + P)
                                last = mm3(GB[t // 2][:, (t % 2) * D:(t % 2) * D + D], PTH[:, j, c], PTL[:, j, c],
                                           XH[s][:, j, :], XL[s][:, j, :], j == 0 and t % 2 == 0, j == NT - 1)
                            if t % 2:
                                last.then_inc(agg_ps[s], 1)
                                if use < USE_L2:
                                    free.by(f"G{t // 2}", (src_ready[s], 2 * NT * use + t + 1))
                                else:
                                    free.by(f"G{t // 2}", (hp_ready[s], NT * (use - USE_L2) + t + 1))
                                yield

                    def forward(s, l):
                        def up(c):
                            free.wait(f"U{c % 2}")
                            for k in range(ND):
                                w = slice(k * HID + c * P, k * HID + c * P + P)
                                last = mm3(U[c % 2][:, :], WH[:, W_UP + l, w], WL[:, W_UP + l, w], *hT(s, k),
                                           k == 0, k == ND - 1)
                            last.then_inc(up_ps[s], 1)
                            free.by(f"U{c % 2}", (g_ready[s], 2 * (NC * l + c + 1)))

                        def down(c):
                            if c == 0:
                                free.wait("Y0")
                                free.wait("Y1")
                            pe.wait_ge(g_ready[s], 2 * (NC * l + c + 1))
                            pe.wait_ge(glo_ready[s], NC * l + c + 1)
                            w = slice(c * D, c * D + D)
                            for t in range(NT):
                                g = slice(t * P, t * P + P)
                                last = mm3(YB[t // 2][:, (t % 2) * D:(t % 2) * D + D], GH[:, c % 2, g], GL[:, c % 2, g],
                                           WH[:, W_DOWN + l, w], WL[:, W_DOWN + l, w], c == 0 and t % 2 == 0, c == NC - 1)
                            last.then_inc(down_done[s], 1)

                        h_ready(s, 2 + 2 * l)
                        for c in range(NC + 2):
                            if c < NC:
                                up(c)
                            if c >= 2:
                                down(c - 2)
                            if c == NC + 1:
                                for i in range(2):
                                    free.by(f"Y{i}", (src_ready[s], 2 * NT * (l + 1)))
                            yield
                        yield
                        yield

                    def dense(s):
                        h_ready(s, 8)
                        for m in range(ND):
                            free.wait(f"U{m}")
                            to_T(U[m], s, W_TAIL, 0, m).then_inc(h2_ps[s], 1)
                            free.by(f"U{m}", (h2_f[s], 2 * (m + 1)))
                        yield
                        pe.wait_ge(h2_f[s], 2 * ND)
                        for t in range(NT):
                            if t % 2 == 0:
                                free.wait(f"G{t // 2}")
                            for c in range(ND):
                                last = nc.tensor.transpose(GB[t // 2][:, (t % 2) * D + c * P:(t % 2) * D + c * P + P],
                                                           tT[:, c, t * P:t * P + P], ident[:, :])
                            if t % 2:
                                last.then_inc(hn_ps[s], 1)
                                free.by(f"G{t // 2}", (xlo_ready[s], USE_L2 + 1))
                        yield
                        pe.wait_ge(h2_lo[s], ND)
                        for m in range(ND):
                            free.wait(f"U{m}")
                            for k in range(ND):
                                last = mm3(U[m][:, :], wblk(WH, W_TAIL, 1, k, m * P, P), wblk(WL, W_TAIL, 1, k, m * P, P),
                                           *hT(s, k), k == 0, k == ND - 1)
                            last.then_inc(ha_ps[s], 1)
                            free.by(f"U{m}", (ha_lo[s], m + 1))
                        yield
                        pe.wait_ge(ha_lo[s], ND)
                        for t in range(NT):
                            free.wait(SCORE[t])
                            c = slice(t * P, t * P + P)
                            for k in range(ND):
                                last = mm3(SB4[t][:, :], HAH[:, k, c], HAL[:, k, c], *hT(s, k), k == 0, k == ND - 1)
                            last.then_inc(s2_ps[s], 1)
                            free.by(SCORE[t], (z_ready[s], NT * USE_L2 + t + 1))
                            if t % 2:
                                yield
                        yield

                    def wh(s):
                        h_ready(s, 9)
                        for i, last in enumerate(to_N(GB, "G", s, W_TAIL, 2)):
                            last.then_inc(hn_ps[s], 1)
                            free.by(f"G{i}", (xlo_ready[s], USE_L3 + 1))
                        yield

                    def idle(n):
                        for _ in range(n):
                            yield

                    def rank1(s, use):
                        yield
                        row_scores(s, use)
                        yield from idle(len(rank1_steps) - 1)

                    def turned(s, u):
                        yield from idle(2)
                        turn(s, u)
                        yield from idle(2)

                    def later(s):
                        yield from idle(2)
                        for l in range(L1N):
                            yield from rank1(s, l)
                            yield from tail(s, l)
                            yield from turned(s, 2 + 2 * l)
                            yield from forward(s, l)
                        yield from turned(s, 8)
                        yield from dense(s)
                        yield from tail(s, USE_L2)
                        yield from idle(2)
                        yield from turned(s, 9)
                        yield from wh(s)
                        yield from rank1(s, USE_L3)
                        yield from tail(s, USE_L3)
                        yield from idle(2)

                    turn(0, 0)
                    project(0)
                    turn(1, 0)
                    heads(0)
                    project(1)
                    heads(1)
                    weave(later)

                @block.scalar
                def _(act):
                    free = Reader(act)

                    def rectified(s, u):
                        v = TURN_OF[u]
                        free.wait(f"hT{s}")
                        for c in range(ND):
                            act.wait_ge(yT_ready[s], ND * v + c + 1)
                            nc.scalar.activation(hT_hi[s][:, c, :], U[c][:, :], ACT.Relu).then_inc(hi_ready[s], 1)

                    def scaled(s, l):
                        v = TURN_OF[2 + 2 * l]
                        free.wait(f"hT{s}")
                        free.wait("tT")
                        for c in range(ND):
                            act.wait_ge(yT_ready[s], ND * v + c + 1)
                            for dst, done in ((tT, t_ready), (hT_hi[s], hi_ready)):
                                nc.scalar.activation(dst[:, c, :], U[c][:, :], ACT.Identity, bias=beta1_col[:, l, c:c + 1],
                                                     scale=g1_col[:, l, c:c + 1]).then_inc(done[s], 1)
                        free.by("tT", (lo_ready[s], ND * v + ND))
                        free.by(f"hT{s}", (down_done[s], NC * (l + 1)))

                    def project(s):
                        for m in range(2):
                            for w in range(2):
                                act.wait_ge(qk_ps[s], 2 * m + w + 1)
                                if s:
                                    act.wait_ge(pv_done[0], 2)
                                nc.scalar.activation(ST[:, w, m, 0, :], U[w][:, :], ACT.Copy).then_inc(qk_hi[s], 1)
                        for i in range(2):
                            act.wait_ge(v_ps[s], i + 1)
                            nc.scalar.activation(V[:, 2 * i:2 * i + 2, :].rearrange("p t d -> p (t d)"), YB[i][:, :],
                                                 ACT.Copy).then_inc(v_ready[s], 1)

                    def heads(s):
                        for i in range(NH + 3):
                            for t in range(NT):
                                if i < NH:
                                    n = i * NT + t
                                    if i >= 3 and t == 0:
                                        act.wait_ge(pt0_ps[s], NT * (i - 2))
                                    elif s and i == 0 and t == 0:
                                        act.wait_ge(pt0_ps[0], NT * NH)
                                    act.wait_ge(z0_ready[s], n + 1)
                                    nc.scalar.activation(PR[:, i % 3, t, :], Z[:, t, :], ACT.Exp, scale=-1.0,
                                                         bias=NMIN[:, s, i, t:t + 1],
                                                         accum_out=RSUM[:, s, i, t:t + 1]).then_inc(p0_ready[s], 1)
                                if 2 <= i < NH + 2 and t % 2 == 0:
                                    h, j = i - 2, t
                                    if h == 0 and t == 0:
                                        for m in range(2):
                                            act.wait_ge(stack_in[m][s], 16 * 6)
                                    if h == HG:
                                        act.wait_ge(pv_done[s], 1)
                                    act.wait_ge(pt0_ps[s], NT * h + j + 1)
                                    nc.scalar.activation(PT[:, h % HG, j, :], U[0][:, :], ACT.Copy).then_inc(pt0_act[s], 1)
                            if i == HG + 2 or i == NH + 2:
                                g = i // HG - 1
                                act.wait_ge(pv_done[s], g + 1)
                                nc.scalar.activation(hT_hi[s][:, g, :], YB[g][:, :], ACT.Relu).then_inc(o_hi[s], 1)
                        free.by(f"hT{s}", (wo_done[s], 2))

                    def upper_x(s, n):
                        act.wait_ge(xn_ready[s], n + 1)
                        if n:
                            act.wait_ge(agg_ps[s], 2 * n)
                        nc.scalar.activation(XH[s][:, :, :], XN[s][:, :, :], ACT.Copy).then_inc(xhi_ready[s], 1)

                    def rank1(s, use):
                        n = use if use < USE_L2 else 3
                        yield from idle(4)
                        act.wait_ge(small_ready[s], n + 1)
                        for t in range(NT):
                            act.wait_ge(z_ready[s], NT * use + t + 1)
                            nc.scalar.activation(PR[:, s, t, :], ZS[s][:, t, :], ACT.Relu, scale=1.0 - SLOPE,
                                                 bias=eb[:, s, 0, t:t + 1]).then_inc(relu_ready[s], 1)
                        yield
                        for t in range(NT):
                            act.wait_ge(w_ready[s], NT * n + t + 1)
                            nc.scalar.activation(PR[:, s, t, :], ZS[s][:, t, :], ACT.Exp, bias=eb[:, s, 1, t:t + 1],
                                                 accum_out=RSUM[:, s, 0, t:t + 1]).then_inc(p_ready[s], 1)
                        yield

                    def tail(s, use):
                        free.wait("PTH")
                        for j in range(NT):
                            act.wait_ge(pt_ps[s], NT * use + j + 1)
                            nc.scalar.activation(PTH[:, j, :], PB[j % 2][:, :], ACT.Copy).then_inc(pt_hi[s], 1)
                            yield
                        free.by("PTH", (agg_ps[s], 2 * (use + 1)))
                        yield from idle(3)

                    def forward(s, l):
                        for c in range(NC):
                            n = NC * l + c
                            act.wait_ge(up_ps[s], n + 1)
                            free.wait(f"GF{c % 2}")
                            for dst in (GF, GH):
                                nc.scalar.activation(dst[:, c % 2, :], U[c % 2][:, :], ACT.Gelu,
                                                     bias=b1_col[:, l, c:c + 1]).then_inc(g_ready[s], 1)
                            free.by(f"GF{c % 2}", (down_done[s], n + 1))
                            yield
                        yield from idle(4)

                    def dense(s):
                        free.wait("tT")
                        free.wait(f"hT{s}")
                        for m in range(ND):
                            act.wait_ge(h2_ps[s], ND)
                            for dst in (tT, hT_hi[s]):
                                nc.scalar.activation(dst[:, m, :], U[m][:, :], ACT.Identity, bias=l2b_col[:, m:m + 1])\
                                    .then_inc(h2_f[s], 1)
                        free.by("tT", (h2_lo[s], ND), (hn_ps[s], 2))
                        free.by(f"hT{s}", (s2_ps[s], NT))
                        yield
                        for i in range(2):
                            act.wait_ge(hn_ps[s], i + 1)
                            nc.scalar.activation(XH[s][:, 2 * i:2 * i + 2, :].rearrange("p t d -> p (t d)"), GB[i][:, :],
                                                 ACT.Copy).then_inc(xhi_ready[s], 1)
                        yield
                        for m in range(ND):
                            act.wait_ge(ha_ps[s], m + 1)
                            nc.scalar.activation(HAH[:, m, :], U[m][:, :], ACT.Copy).then_inc(ha_hi[s], 1)
                        yield
                        yield
                        for t in range(NT):
                            act.wait_ge(z_ready[s], NT * USE_L2 + t + 1)
                            nc.scalar.activation(PR[:, s, t, :], ZS[s][:, t, :], ACT.Exp, scale=-1.0,
                                                 bias=NMIN[:, s, 0, t:t + 1],
                                                 accum_out=RSUM[:, s, 0, t:t + 1]).then_inc(p_ready[s], 1)
                            if t % 2:
                                yield

                    def wh(s):
                        for i in range(2):
                            act.wait_ge(hn_ps[s], 3 + i)
                            for dst, done in ((XN[s], xn_ready), (XH[s], xhi_ready)):
                                nc.scalar.activation(dst[:, 2 * i:2 * i + 2, :].rearrange("p t d -> p (t d)"),
                                                     GB[i][:, :], ACT.Copy).then_inc(done[s], 1)
                        yield

                    def elu(s, i):
                        act.wait_ge(mn_ready[s], i + 1)
                        nc.scalar.activation(RES[s][:, :, :], RES[s][:, :, :], ACT.Exp).then_inc(ex_ready[s], 1)
                        yield from idle(2)

                    def idle(n):
                        for _ in range(n):
                            yield

                    def later(s):
                        yield from idle(2)
                        for l in range(L1N):
                            upper_x(s, l)
                            yield from rank1(s, l)
                            yield from tail(s, l)
                            yield from idle(2)
                            scaled(s, l)
                            yield from idle(2)
                            yield from forward(s, l)
                        yield from idle(2)
                        rectified(s, 8)
                        free.by(f"hT{s}", (h2_ps[s], ND))
                        yield from idle(2)
                        yield from dense(s)
                        yield from tail(s, USE_L2)
                        yield from elu(s, 0)
                        yield from idle(2)
                        rectified(s, 9)
                        yield from idle(2)
                        yield from wh(s)
                        yield from rank1(s, USE_L3)
                        yield from tail(s, USE_L3)
                        yield from elu(s, 1)

                    rectified(0, 0)
                    project(0)
                    rectified(1, 0)
                    heads(0)
                    project(1)
                    heads(1)
                    weave(later)

                @block.vector
                def _(dve):
                    free = Reader(dve)
                    v = nc.vector

                    def masks(s):
                        dve.wait_ge(adj_in[s], 16)
                        v.tensor_scalar(mask[s][:, :, :, :],
                                        adj_stage[s].bitcast(I32).rearrange("p t (q j) -> p t j q", j=NT),
                                        0.0, MASKED, ALU.is_equal, ALU.mult).then_inc(mask_ready[s], 1)
                        dve.wait_ge(mask_ready[s], 1)
                        v.tensor_copy(mask_self[s][:, :, :, :], mask[s][:, :, :, :]).then_inc(mask_ready[s], 1)

                    def statistics(s, u, src):
                        for t in range(NT):
                            v.bn_stats(stats[:, s, t, :], src[:, t, :]).then_inc(stat_done[s], 1)
                        for t in range(NT):
                            dve.wait_ge(stat_done[s], 2 * NT * u + t + 1)
                            v.bn_aggr(mv[:, s, t, :], stats[:, s, t, :]).then_inc(stat_done[s], 1)
                        dve.wait_ge(stat_done[s], 2 * NT * (u + 1))
                        v.tensor_scalar(ve[:, s, :], mv[:, s, :, 1], EPS, None, ALU.add).then_inc(var_ready[s], 1)

                    def norm(s, u, src):
                        dve.wait_ge(rstd_ready[s], u + 1)
                        free.wait("Y")
                        for t in range(NT):
                            v.tensor_scalar(Y[:, t, :], src[:, t, :], mv[:, s, t, 0:1], rstd[:, s, t:t + 1],
                                            ALU.subtract, ALU.mult).then_inc(y_ready[s], 1)
                        if u in TURN_OF:
                            n = ND * (TURN_OF[u] + 1)
                            if u in (2, 4, 6):
                                free.by("Y", (yT_ready[s], n), (res_ready[s], u - 1))
                            else:
                                free.by("Y", (yT_ready[s], n))

                    def rectified(s, u):
                        n = ND * TURN_OF[u]
                        for c in range(ND):
                            dve.wait_ge(hi_ready[s], n + c + 1)
                            v.scalar_tensor_tensor(hT_lo[s][:, c, :], U[c][:, :], 0.0, hT_hi[s][:, c, :],
                                                   ALU.max, ALU.subtract).then_inc(lo_ready[s], 1)

                    def scaled(s, l):
                        n = ND * TURN_OF[2 + 2 * l]
                        for c in range(ND):
                            dve.wait_ge(hi_ready[s], n + c + 1)
                            dve.wait_ge(t_ready[s], ND * l + c + 1)
                            v.tensor_tensor(hT_lo[s][:, c, :], tT[:, c, :], hT_hi[s][:, c, :], ALU.subtract)\
                                .then_inc(lo_ready[s], 1)

                    def project(s):
                        for m in range(2):
                            for w in range(2):
                                dve.wait_ge(qk_hi[s], 2 * m + w + 1)
                                v.tensor_tensor(ST[:, w, m, 1, :], U[w][:, :], ST[:, w, m, 0, :], ALU.subtract)\
                                    .then_inc(qk_lo[s], 1)

                    def heads(s):
                        for i in range(NH + 3):
                            for t in range(NT):
                                if i < NH:
                                    n = i * NT + t
                                    dve.wait_ge(s0_ready[s], n + 1)
                                    if i:
                                        dve.wait_ge(p0_ready[s], n - NT + 1)
                                    v.tensor_tensor_reduce(
                                        out=Z[:, t, :], in0=SB4[t][:, :],
                                        in1=mask[s][:, t, :, :].rearrange("p j q -> p (j q)"), scale=NEG_SCALE,
                                        scalar=3e38, op0=ALU.add, op1=ALU.min,
                                        accum_out=NMIN[:, s, i, t:t + 1]).then_inc(z0_ready[s], 1)
                                if t == 1 and 1 <= i <= NH:
                                    dve.wait_ge(p0_ready[s], NT * i)
                                    v.reciprocal(RINV[:, s, i - 1, :], RSUM[:, s, i - 1, :]).then_inc(r0_ready[s], 1)
                                if 2 <= i < NH + 2 and t % 2:
                                    h, j = i - 2, t
                                    if h == 0 and t == 1:
                                        for m in range(2):
                                            dve.wait_ge(stack_in[m][s], 16 * 6)
                                    if h == HG:
                                        dve.wait_ge(pv_done[s], 1)
                                    dve.wait_ge(pt0_ps[s], NT * h + j + 1)
                                    v.tensor_copy(PT[:, h % HG, j, :], U[1][:, :]).then_inc(pt0_dve[s], 1)
                            if i == HG + 2 or i == NH + 2:
                                g = i // HG - 1
                                dve.wait_ge(o_hi[s], g + 1)
                                v.scalar_tensor_tensor(hT_lo[s][:, g, :], YB[g][:, :], 0.0, hT_hi[s][:, g, :],
                                                       ALU.max, ALU.subtract).then_inc(o_lo[s], 1)
                        for i in range(2):
                            dve.wait_ge(wo_done[s], i + 1)
                            xs = X[s][:, 2 * i:2 * i + 2, :].rearrange("p t d -> p (t d)")
                            v.tensor_tensor(xs, xs, GB[i][:, :], ALU.add).then_inc(x1_ready[s], 1)

                    def rank1(s, use):
                        n = use if use < USE_L2 else 3
                        si, sj, c, top, u1, u2 = (sml[:, s, i, :] for i in range(6))
                        dve.wait_ge(xn_ready[s], use + 1 if use < USE_L2 else L1N + 3)
                        for t in range(NT):
                            for dst, a in ((sj, 1), (si, 0)):
                                v.tensor_tensor_reduce(out=ZS[s][:, t, a * D:a * D + D], in0=XN[s][:, t, :],
                                                       in1=a_bc[:, n, a, :], scale=1.0, scalar=0.0, op0=ALU.mult,
                                                       op1=ALU.add, accum_out=dst[:, t:t + 1]).then_inc(dot_done[s], 1)
                            if t == 1:
                                yield
                        free.wait("diag")
                        for t in range(NT):
                            dve.wait_ge(dot_done[s], 2 * NT * n + 2 * t + 2)
                            v.tensor_scalar(diag[:, t, :], ident[:, :], sj[:, t:t + 1], None, ALU.mult)\
                                .then_inc(diag_ready[s], 1)
                        free.by("diag", (sj_ready[s], n + 1))
                        v.tensor_scalar(c, si, ab_bc[:, n:n + 1], None, ALU.add).then_inc(small_done[s], 1)
                        yield
                        m = mask_self if use < USE_L2 else mask
                        if use < USE_L2:
                            dve.wait_ge(self_ready[s], NT)
                        dve.wait_ge(sj_ready[s], n + 1)
                        for t in range(NT):
                            v.tensor_tensor_reduce(out=ZS[s][:, t, :], in0=PB[0][:, :],
                                                   in1=m[s][:, t, :, :].rearrange("p j q -> p (j q)"), scale=1.0,
                                                   scalar=-3e38, op0=ALU.add, op1=ALU.max,
                                                   accum_out=top[:, t:t + 1]).then_inc(z_ready[s], 1)
                            if t == 1:
                                yield
                        k = 5 * n
                        dve.wait_ge(small_done[s], k + 1)
                        v.tensor_scalar(eb[:, s, 0, :], c, 1.0 - SLOPE, None, ALU.mult).then_inc(small_done[s], 1)
                        dve.wait_ge(z_ready[s], NT * (use + 1))
                        v.tensor_tensor(u1, top, c, ALU.add).then_inc(small_done[s], 1)
                        dve.wait_ge(small_done[s], k + 3)
                        v.scalar_tensor_tensor(u2, u1, SLOPE, u1, ALU.mult, ALU.max).then_inc(small_done[s], 1)
                        dve.wait_ge(small_done[s], k + 4)
                        v.scalar_tensor_tensor(eb[:, s, 1, :], c, SLOPE, u2, ALU.mult, ALU.subtract)\
                            .then_inc(small_done[s], 1)
                        dve.wait_ge(small_done[s], k + 5)
                        v.tensor_copy(sml[:, s, 7, :], eb[:, s, 1, :]).then_inc(small_ready[s], 1)
                        yield
                        for t in range(NT):
                            dve.wait_ge(relu_ready[s], NT * n + t + 1)
                            v.scalar_tensor_tensor(ZS[s][:, t, :], ZS[s][:, t, :], SLOPE, PR[:, s, t, :],
                                                   ALU.mult, ALU.add).then_inc(w_ready[s], 1)
                            if t % 2:
                                yield

                    def tail(s, use, taken):
                        yield
                        for j in range(NT):
                            dve.wait_ge(pt_hi[s], NT * use + j + 1)
                            v.tensor_tensor(PTL[:, j, :], PB[j % 2][:, :], PTH[:, j, :], ALU.subtract)\
                                .then_inc(pt_lo[s], 1)
                            if j == NT - 1:
                                dve.wait_ge(p_ready[s], NT * (use + 1))
                                v.reciprocal(RINV[:, s, 0, :], RSUM[:, s, 0, :]).then_inc(rinv_ready[s], 1)
                            yield
                        yield
                        dve.wait_ge(rinv_ready[s], use + 1)
                        taken(0)
                        yield

                    def aggregated(s, l):
                        def half(i):
                            dve.wait_ge(agg_ps[s], 2 * l + i + 1)
                            for t in (2 * i, 2 * i + 1):
                                v.scalar_tensor_tensor(XN[s][:, t, :], GB[i][:, (t % 2) * D:(t % 2) * D + D],
                                                       RINV[:, s, 0, t:t + 1], XN[s][:, t, :], ALU.mult, ALU.add)\
                                    .then_inc(src_ready[s], 1)
                        return half

                    def forward(s, l):
                        for c in range(NC + 1):
                            if c:
                                n = NC * l + c - 1
                                dve.wait_ge(g_ready[s], 2 * n + 2)
                                free.wait(f"GL{n % 2}")
                                v.tensor_tensor(GL[:, n % 2, :], GF[:, n % 2, :], GH[:, n % 2, :], ALU.subtract)\
                                    .then_inc(glo_ready[s], 1)
                                free.by(f"GL{n % 2}", (down_done[s], n + 1))
                            yield
                        yield
                        dve.wait_ge(down_done[s], NC * (l + 1))
                        dve.wait_ge(res_ready[s], 2 * l + 2)
                        for t in range(NT):
                            v.tensor_tensor(XN[s][:, t, :], YB[t // 2][:, (t % 2) * D:(t % 2) * D + D], RES[s][:, t, :],
                                            ALU.add).then_inc(src_ready[s], 1)
                        dve.wait_ge(src_ready[s], 2 * NT * l + 2 * NT)
                        statistics(s, 3 + 2 * l, XN[s])
                        yield
                        norm(s, 3 + 2 * l, XN[s])
                        dve.wait_ge(y_ready[s], NT * (4 + 2 * l))
                        v.tensor_tensor(XN[s][:, :, :], Y[:, :, :], g2_bc[:, l:l + 1, :].to_broadcast([P, NT, D]),
                                        ALU.mult).then_inc(half_done[s], 1)
                        dve.wait_ge(half_done[s], l + 1)
                        v.tensor_tensor(XN[s][:, :, :], XN[s][:, :, :], beta2_bc[:, l:l + 1, :].to_broadcast([P, NT, D]),
                                        ALU.add).then_inc(xn_ready[s], 1)
                        if l == L1N - 1:
                            dve.wait_ge(xn_ready[s], L1N + 1)
                            v.tensor_tensor(X[s][:, :, :], X[s][:, :, :], XN[s][:, :, :], ALU.add)\
                                .then_inc(xs_ready[s], 1)
                        yield

                    def lower_x(s, n):
                        for i in range(2):
                            dve.wait_ge(xhi_ready[s], n + i + 1)
                            c = slice(2 * i, 2 * i + 2)
                            last = v.tensor_tensor(XL[s][:, c, :].rearrange("p t d -> p (t d)"), GB[i][:, :],
                                                   XH[s][:, c, :].rearrange("p t d -> p (t d)"), ALU.subtract)
                        last.then_inc(xlo_ready[s], 1)

                    def dense(s):
                        yield
                        for m in range(ND):
                            dve.wait_ge(h2_f[s], 2 * (m + 1))
                            v.tensor_tensor(hT_lo[s][:, m, :], tT[:, m, :], hT_hi[s][:, m, :], ALU.subtract)\
                                .then_inc(h2_lo[s], 1)
                        yield
                        lower_x(s, L1N)
                        yield
                        for m in range(ND):
                            dve.wait_ge(ha_hi[s], m + 1)
                            v.tensor_tensor(HAL[:, m, :], U[m][:, :], HAH[:, m, :], ALU.subtract).then_inc(ha_lo[s], 1)
                        yield
                        for t in range(NT):
                            dve.wait_ge(s2_ps[s], t + 1)
                            v.tensor_tensor_reduce(out=ZS[s][:, t, :], in0=SB4[t][:, :],
                                                   in1=mask[s][:, t, :, :].rearrange("p j q -> p (j q)"), scale=-1.0,
                                                   scalar=3e38, op0=ALU.add, op1=ALU.min,
                                                   accum_out=NMIN[:, s, 0, t:t + 1]).then_inc(z_ready[s], 1)
                            if t % 2:
                                yield

                    def scaled_out(s, i):
                        def half(k):
                            dve.wait_ge(agg_ps[s], 2 * (USE_L2 + i) + k + 1)
                            for t in (2 * k, 2 * k + 1):
                                v.tensor_scalar(XN[s][:, t, :], GB[k][:, (t % 2) * D:(t % 2) * D + D],
                                                RINV[:, s, 0, t:t + 1], None, ALU.mult).then_inc(hp_ready[s], 1)
                        return half

                    def elu(s, i):
                        scaled_out(s, i)(1)
                        dve.wait_ge(hp_ready[s], NT * (i + 1))
                        v.tensor_scalar(RES[s][:, :, :], XN[s][:, :, :], 0.0, None, ALU.min).then_inc(mn_ready[s], 1)
                        yield
                        dve.wait_ge(ex_ready[s], i + 1)
                        v.scalar_tensor_tensor(XN[s][:, :, :], XN[s][:, :, :], 0.0, RES[s][:, :, :], ALU.max, ALU.add)\
                            .then_inc(el_ready[s], 1)
                        dve.wait_ge(el_ready[s], i + 1)
                        v.scalar_tensor_tensor(X[s][:, :, :], XN[s][:, :, :], -1.0, X[s][:, :, :], ALU.add, ALU.add)\
                            .then_inc(xs_ready[s], 1)
                        yield

                    def enter(s, u, ready, n):
                        dve.wait_ge(ready[s], n)
                        statistics(s, u, X[s])
                        yield
                        norm(s, u, X[s])
                        yield
                        if u in TURN_OF:
                            yield
                            rectified(s, u)
                            yield

                    def later(s):
                        dve.wait_ge(x1_ready[s], 2)
                        statistics(s, 1, X[s])
                        yield
                        norm(s, 1, X[s])
                        dve.wait_ge(y_ready[s], NT * 2)
                        v.tensor_scalar(XN[s][:, :, :], Y[:, :, :], 0.0, None, ALU.max).then_inc(xn_ready[s], 1)
                        yield
                        for l in range(L1N):
                            yield from rank1(s, l)
                            yield from tail(s, l, aggregated(s, l))
                            aggregated(s, l)(1)
                            dve.wait_ge(src_ready[s], 2 * NT * l + NT)
                            statistics(s, 2 + 2 * l, XN[s])
                            yield
                            norm(s, 2 + 2 * l, XN[s])
                            yield
                            yield
                            scaled(s, l)
                            yield
                            yield from forward(s, l)
                        yield from enter(s, 8, xs_ready, 1)
                        yield from dense(s)
                        yield from tail(s, USE_L2, scaled_out(s, 0))
                        yield from elu(s, 0)
                        yield from enter(s, 9, xs_ready, 2)
                        yield
                        lower_x(s, L1N + 2)
                        yield from rank1(s, USE_L3)
                        yield from tail(s, USE_L3, scaled_out(s, 1))
                        yield from elu(s, 1)

                    for s in range(STREAMS):
                        masks(s)
                        dve.wait_ge(x_in[s], 16)
                        statistics(s, 0, X[s])
                        norm(s, 0, X[s])
                        rectified(s, 0)
                        if s == 0:
                            project(0)
                    heads(0)
                    project(1)
                    heads(1)
                    weave(later)
            nc.all_engine_barrier(sems_to_clear=sems)


_INS = ["x", "adj", "L0_gnn_Wq", "L0_gnn_Wk", "L0_gnn_Wv", "L0_gnn_Wo", "L1_gnn_attn_w", "L1_gnn_attn_b",
        "L1_gnn_W1", "L1_gnn_b1", "L1_gnn_W2", "L1_gnn_b2", "L1_gnn_g1", "L1_gnn_beta1", "L1_gnn_g2",
        "L1_gnn_beta2", "L2_gnn_W", "L2_gnn_b", "L2_gnn_attn", "L3_gnn_W", "L3_gnn_a"]


def kernel(**inputs):
    import numpy as np
    import concourse.bacc as bacc
    from concourse.bass_utils import run_bass_kernel_spmd

    nc = bacc.Bacc("TRN2", target_bir_lowering=False, num_devices=1)
    arrays, args = {}, []
    for name in _INS:
        a = np.ascontiguousarray(inputs[name])
        arrays[f"in_{name}"] = a
        args.append(nc.dram_tensor(f"in_{name}", a.shape, mybir.dt.from_np(a.dtype), kind="ExternalInput").ap())
    args.append(nc.dram_tensor("out", (B, N, D), F32, kind="ExternalOutput").ap())
    build(nc, *args)
    r = run_bass_kernel_spmd(nc, [arrays], core_ids=[0])
    return r.results[0]["out"]
```

```python
from contextlib import ExitStack

import concourse.bass as bass
from concourse import mybir

F32 = mybir.dt.float32
F16 = mybir.dt.float16
BF16 = mybir.dt.bfloat16
I32 = mybir.dt.int32
ALU = mybir.AluOpType
ACT = mybir.ActivationFunctionType

P = 128
B, N, D = 16, 512, 256
NT = N // P
ND = D // P
NH, DK = 8, 32
HG = P // DK
L1N = 3
HID = 4 * D
NC = HID // P
EPS = 1e-5
MASKED = -1e30
NEG_SCALE = -float(DK) ** -0.5
SLOPE = 0.2
STREAMS = 2

W_L0, W_TAIL, W_UP, W_DOWN = 0, 1, 2, 5
NBLK = 8
USE_L2, USE_L3 = 3, 4
TURN_OF = {0: 0, 2: 1, 4: 2, 6: 3, 8: 4, 9: 5}
BEFORE_LOOP = -1

ORDER = ("22202002200000010100101111100110101010010010000011011101011100010100110100100111",
         "11010110101010100001000011011101111000000111010100101011110101101001010100000100",
         "11011100111110110010010001010010100110001110111010111101011001101001001000001100",
         "1011111131313131333")


def norm_no(s, u):
    return 0 if u == BEFORE_LOOP else u if s else (u - 1) % 10


def turn_no(s, u):
    return 0 if u == BEFORE_LOOP else TURN_OF[u] if s else (TURN_OF[u] - 1) % len(TURN_OF)


def build(nc, x, adj, Wq, Wk, Wv, Wo, attn_w, attn_b, W1, b1, W2, b2, g1, beta1, g2, beta2,
          L2W, L2b, L2attn, L3W, L3a, out):
    ctx = ExitStack()
    with ctx:
        def sb(name, shape, dt):
            return ctx.enter_context(nc.sbuf_tensor(name, shape, dt))

        WH = sb("weights_hi", [P, NBLK, 2048], F16)
        WL = sb("weights_lo", [P, NBLK, 2048], F16)
        ident = sb("ident", [P, P], F32)
        ones = sb("ones", [P, P], F32)
        minus_half = sb("minus_half", [P, NT], F32)
        g1_bc = sb("g1_bc", [P, L1N, D], F32)
        res_bc = sb("beta1_b2_bc", [P, L1N, D], F32)
        g2_bc = sb("g2_bc", [P, L1N, D], F32)
        beta2_bc = sb("beta2_bc", [P, L1N, D], F32)
        a_bc = sb("a_bc", [P, L1N + 1, 2, D], F32)
        ab_bc = sb("attn_b_bc", [P, L1N + 1], F32)
        g1_col = sb("g1_col", [P, L1N, ND], F32)
        beta1_col = sb("beta1_col", [P, L1N, ND], F32)
        b1_col = sb("b1_col", [P, L1N, NC], F32)
        l2b_col = sb("l2b_col", [P, ND], F32)
        X = [sb(f"x{s}", [P, NT, D], F32) for s in range(2)]
        mask = [sb(f"mask{s}", [P, NT, NT, P], BF16) for s in range(2)]
        mask_self = [sb(f"mask_self{s}", [P, NT, NT, P], BF16) for s in range(2)]
        Y = sb("y", [P, NT, D], F32)
        hT_hi = [sb(f"hT_hi{s}", [P, ND, N], F16) for s in range(2)]
        hT_lo = [sb(f"hT_lo{s}", [P, ND, N], F16) for s in range(2)]
        tT = sb("tT", [P, ND, N], F32)
        Z = sb("z", [P, NT, N], F32)
        PR = sb("probs", [P, 3, NT, N], F32)
        V = [tT[:, :, :].rearrange("p c (a d) -> p (c a) d", a=2), Y[:, :, :]]
        arena = sb("arena", [P, 12288], F32)
        PT = arena[:, 0:8192].rearrange("p (h j n) -> p h j n", h=HG, j=NT)
        ST = [arena[:, 6144 * s:6144 * s + 2048].bitcast(F16).rearrange("p (w m e n) -> p w m e n", w=2, m=2, e=2)
              for s in range(2)]
        QS = arena[:, 8192:10240].bitcast(F16).rearrange("p (h n) -> p h n", h=NH)
        KS = arena[:, 10240:12288].bitcast(F16).rearrange("p (h n) -> p h n", h=NH)
        XN = [arena[:, 8192 + 1024 * s:9216 + 1024 * s].rearrange("p (t d) -> p t d", t=NT) for s in range(2)]
        RES = [arena[:, 2048 + 1024 * s:3072 + 1024 * s].rearrange("p (t d) -> p t d", t=NT) for s in range(2)]
        XHL = [arena[:, 10240:11264], arena[:, 4096:5120]]
        XH = [m[:, 0:512].bitcast(F16).rearrange("p (t d) -> p t d", t=NT) for m in XHL]
        XL = [m[:, 512:1024].bitcast(F16).rearrange("p (t d) -> p t d", t=NT) for m in XHL]
        HAH = arena[:, 5120:5632].bitcast(F16).rearrange("p (m n) -> p m n", m=ND)
        HAL = arena[:, 5632:6144].bitcast(F16).rearrange("p (m n) -> p m n", m=ND)
        PTH = arena[:, 6144:7168].bitcast(F16).rearrange("p (j n) -> p j n", j=NT)
        PTL = arena[:, 7168:8192].bitcast(F16).rearrange("p (j n) -> p j n", j=NT)
        GF = arena[:, 0:1024].rearrange("p (r n) -> p r n", r=2)
        GH = arena[:, 1024:1536].bitcast(F16).rearrange("p (r n) -> p r n", r=2)
        GL = arena[:, 1536:2048].bitcast(F16).rearrange("p (r n) -> p r n", r=2)
        diag = arena[:, 11264:11776].rearrange("p (t n) -> p t n", t=NT)
        ZS = [Z, PR[:, 2, :, :]]
        NMIN = sb("nmin", [P, 2, NH, NT], F32)
        RSUM = sb("rsum", [P, 2, NH, NT], F32)
        RINV = sb("rinv", [P, 2, NH, NT], F32)
        stats = sb("stats", [P, 2, NT, 6], F32)
        mv = sb("mv", [P, 2, NT, 2], F32)
        ve = sb("ve", [P, 2, NT], F32)
        rstd = sb("rstd", [P, 2, NT], F32)
        sml = sb("small", [P, 2, 8, NT], F32)
        eb = sb("eb", [P, 2, 2, NT], F32)
        U = [ctx.enter_context(nc.psum_tensor(f"U{i}", [P, 512], F32)) for i in range(2)]
        YB = [ctx.enter_context(nc.psum_tensor(f"Y{i}", [P, 512], F32)) for i in range(2)]
        PB = [ctx.enter_context(nc.psum_tensor(f"P{i}", [P, 512], F32)) for i in range(2)]
        GB = [ctx.enter_context(nc.psum_tensor(f"G{i}", [P, 512], F32)) for i in range(2)]
        SB4, SCORE = [PB[0], PB[1], GB[0], GB[1]], ["P0", "P1", "G0", "G1"]

        def sem(name):
            return ctx.enter_context(nc.semaphore(name))

        def per_stream(name):
            return [sem(f"{name}{s}") for s in range(STREAMS)]

        loaded = [sem(f"loaded{i}") for i in range(NBLK)]
        split, wT = sem("split"), sem("wT")
        const_ready, ident_ready = sem("const_ready"), sem("ident_ready")
        x_in, adj_in = per_stream("x_in"), per_stream("adj_in")
        mask_ready, self_ready = per_stream("mask_ready"), per_stream("self_ready")
        stat_done, var_ready, rstd_ready = (per_stream(n) for n in ("stat", "var", "rstd"))
        y_ready, yT_ready, hi_ready, lo_ready, t_ready = (per_stream(n) for n in ("y", "yT", "hT_hi", "hT_lo", "tT"))
        qk_ps, qk_hi, qk_lo = per_stream("qk_ps"), per_stream("qk_hi"), per_stream("qk_lo")
        stack_in = [[sem(f"stack{m}_{s}") for s in range(2)] for m in range(2)]
        v_ps, v_ready = per_stream("v_ps"), per_stream("v_sb")
        s0_ready, z0_ready, p0_ready, r0_ready, pn_ready, pt0_ps, pt0_act, pt0_dve, pv_done = (
            per_stream(n) for n in ("s0", "z0", "p0", "r0", "pn", "pt0", "pt0_act", "pt0_dve", "pv"))
        o_hi, o_lo, wo_done, x1_ready = (per_stream(n) for n in ("o_hi", "o_lo", "wo", "x1"))
        dot_done, diag_ready, sj_ready, z_ready, small_done, small_ready = (
            per_stream(n) for n in ("dot", "diag", "sj", "z", "small", "bias"))
        relu_ready, w_ready, p_ready, pt_ps, pt_hi, pt_lo, agg_ps, rinv_ready = (
            per_stream(n) for n in ("relu", "w", "p", "pt", "pt_hi", "pt_lo", "agg", "rinv"))
        xn_ready, xhi_ready, xlo_ready, src_ready, res_ready = (
            per_stream(n) for n in ("xn", "x_hi", "x_lo", "src", "res"))
        up_ps, g_ready, glo_ready, down_done = (per_stream(n) for n in ("up", "g", "g_lo", "down"))
        h2_ps, h2_f, h2_lo, ha_ps, ha_hi, ha_lo, hn_ps, s2_ps = (
            per_stream(n) for n in ("h2_ps", "h2_f", "h2_lo", "ha_ps", "ha_hi", "ha_lo", "hn_ps", "s2"))
        hp_ready, mn_ready, ex_ready, el_ready, xs_ready = (per_stream(n) for n in ("hp", "mn", "ex", "el", "xs"))
        half_done = per_stream("x_half")
        bounced = per_stream("bounced")
        stored = per_stream("stored")
        sems = range(loaded[0].num, stored[-1].num + 1)

        adj_stage = [Z[:, :, :], PR[:, 0, :, :]]
        bounce = nc.dram_tensor("qk_parts", (STREAMS, 2, 2, P, 2, N), F16).ap()

        def fetch(sp, turn):
            def load(dst, src, s, done):
                sp.dma_start(dst, src[bass.ds(turn * STREAMS + s, 1), :, :].rearrange("b (p t) d -> p (b t) d", t=NT))\
                  .then_inc(done, 16)
            load(X[0][:, :, :], x, 0, x_in[0])
            for s in range(STREAMS):
                load(adj_stage[s].bitcast(I32), adj, s, adj_in[s])

        def store_second(eng, turn):
            eng.dma_start(out[bass.ds(turn * STREAMS + 1, 1), :, :].rearrange("b (p t) d -> p (b t) d", t=NT),
                          X[1][:, :, :]).then_inc(stored[1], 16)
            eng.wait_ge(stored[1], 16)

        def bounce_out(sp, s):
            for m in range(2):
                for w in range(2):
                    sp.wait_ge(qk_lo[s], 2 * m + w + 1)
                    sp.dma_start(bounce[s, m, w], ST[s][:, w, m, :, :]).then_inc(bounced[s], 16)

        class Reader:

            def __init__(self, eng):
                self.eng, self.at = eng, {}

            def wait(self, buf):
                for at in self.at.pop(buf, ()):
                    self.eng.wait_ge(*at)

            def by(self, buf, *ats):
                self.at[buf] = ats

        def steps(*places):
            return list(places)

        rank1_steps = steps("", "P", "P", "P", "", "")
        tail_steps = steps("PTG", "PTG", "PTG", "PTG", "PTG", "TG")
        norm_steps = steps("", "N")
        turn_steps = steps("NXU", "XU")
        forward_steps = steps("F", "F", *["FY"] * (NC - 2), "FY", "FY", "Y", "N")
        dense_steps = steps("XU", "XG", "GUH", "PGUH", "PGH", "PG")
        elu_steps = steps("", "")
        wh_steps = steps("G")

        def holding_g(these):
            return [these[0] + "G"] + these[1:]

        thread = steps("", "") + L1N * (rank1_steps + tail_steps + holding_g(norm_steps) + turn_steps + forward_steps) \
            + norm_steps + turn_steps + dense_steps + tail_steps + holding_g(elu_steps) \
            + norm_steps + turn_steps + wh_steps + holding_g(rank1_steps) + tail_steps + holding_g(elu_steps)
        heads_steps = steps("", "", "", "NP", "NP", "NP")
        front_steps = steps("", "N", "NU", "U", "U", "U", "Y")
        threads, done = [thread, thread, heads_steps, front_steps], [0, 0, 0, 0]
        order = [int(c) for row in ORDER for c in row]
        for s in order:
            after = {0: done[2] > 0, 1: done[2] == len(heads_steps), 2: True, 3: done[0] == len(thread)}
            assert after[s]
            for o in range(len(threads)):
                k = done[o]
                if o != s and 0 < k < len(threads[o]):
                    assert not set(threads[o][k - 1]) & set(threads[o][k]) & set(threads[s][done[s]])
            done[s] += 1
        assert done == [len(t) for t in threads]

        def weave(later, heads, front):
            threads = [later(s) for s in range(STREAMS)] + [heads(), front()]
            for s in order:
                next(threads[s])
            assert all(next(t, None) is None for t in threads)

        def wblk(W, blk, w, k, c0, n):
            return W[:, blk, w * 512 + k * D + c0:w * 512 + k * D + c0 + n]

        WEIGHED_AT = [HG * (g + 1) + 2 for g in range(STREAMS * NH // HG)]
        LAST_HEAD_STEP = WEIGHED_AT[-1]
        FIRST_WOVEN = LAST_HEAD_STEP + 2 - len(heads_steps)
        OUTPUT_AT = WEIGHED_AT[1] + 2

        def evacuate(eng, i, j):
            s, h = divmod(i, NH)
            if i == HG - 1:
                eng.wait_ge(bounced[1], 16 * 4)
            if i >= HG and h % HG == 0:
                u, g = divmod(i // HG - 1, 2)
                eng.wait_ge(pv_done[u], NT * g + j + 1)
            eng.wait_ge(pt0_ps[s], NT * h + j + 1)

        def front_banks(s, u=0):
            return (YB, "Y") if s and u == 0 else (U, "U")

        def idle(n):
            for _ in range(n):
                yield

        def pool_parts(pool):
            def self_mask(s):
                pool.wait_ge(mask_ready[s], 2)
                for t in range(NT):
                    nc.gpsimd.affine_select(out=mask_self[s][:, t, t, :], in_=mask_self[s][:, t, t, :],
                                            compare_op=ALU.not_equal, fill=0.0, base=0, pattern=[[-1, P]],
                                            channel_multiplier=1).then_inc(self_ready[s], 1)

            def norm(s, u):
                pool.wait_ge(var_ready[s], norm_no(s, u) + 1)
                nc.gpsimd.tensor_tensor(rstd[:, s, :], ve[:, s, :], minus_half[:, :], ALU.pow)\
                    .then_inc(rstd_ready[s], 1)

            return self_mask, norm

        def tensor_parts(pe, free):
            def mm3(dst, ah, al, bh, bl, start, stop):
                nc.tensor.matmul(dst, ah, bh, start=start, stop=False, skip_group_check=True)
                nc.tensor.matmul(dst, ah, bl, start=False, stop=False, skip_group_check=True)
                return nc.tensor.matmul(dst, al, bh, start=False, stop=stop, skip_group_check=True)

            def turn(s, u):
                v = turn_no(s, u)
                pe.wait_ge(y_ready[s], NT * (norm_no(s, u) + 1))
                banks, name = front_banks(s, u)
                for c in range(ND):
                    free.wait(f"{name}{c}")
                    for t in range(NT):
                        last = nc.tensor.transpose(banks[c][:, t * P:t * P + P], Y[:, t, c * P:c * P + P], ident[:, :])
                    last.then_inc(yT_ready[s], 1)
                    free.by(f"{name}{c}", (lo_ready[s], ND * v + c + 1))

            def h_ready(s, u):
                pe.wait_ge(hi_ready[s], ND * (turn_no(s, u) + 1))
                pe.wait_ge(lo_ready[s], ND * (turn_no(s, u) + 1))

            def hT(s, k, c0=0, n=N):
                return hT_hi[s][:, k, c0:c0 + n], hT_lo[s][:, k, c0:c0 + n]

            def to_T(bank, s, blk, w, m):
                for k in range(ND):
                    last = mm3(bank[:, :], wblk(WH, blk, w, k, m * P, P), wblk(WL, blk, w, k, m * P, P),
                               *hT(s, k), k == 0, k == ND - 1)
                return last

            def to_N(banks, name, s, blk, w):
                for t in range(NT):
                    if t % 2 == 0:
                        free.wait(f"{name}{t // 2}")
                    for k in range(ND):
                        last = mm3(banks[t // 2][:, (t % 2) * D:(t % 2) * D + D], *hT(s, k, t * P, P),
                                   wblk(WH, blk, w, k, 0, D), wblk(WL, blk, w, k, 0, D),
                                   k == 0 and t % 2 == 0, k == ND - 1)
                    if t % 2:
                        yield last

            def project_qk(s, m):
                banks, name = front_banks(s)
                for w in range(2):
                    free.wait(f"{name}{w}")
                    to_T(banks[w], s, W_L0, w, m).then_inc(qk_ps[s], 1)
                    free.by(f"{name}{w}", (qk_lo[s], 2 * m + w + 1))

            def project_v(s):
                for i, last in enumerate(to_N(YB, "Y", s, W_L0, 2)):
                    last.then_inc(v_ps[s], 1)
                    free.by(f"Y{i}", (v_ready[s], i + 1))

            return mm3, turn, h_ready, hT, to_T, to_N, project_qk, project_v

        def scalar_parts(act, free):
            def rectified(s, u):
                v = turn_no(s, u)
                free.wait(f"hT{s}")
                for c in range(ND):
                    act.wait_ge(yT_ready[s], ND * v + c + 1)
                    nc.scalar.activation(hT_hi[s][:, c, :], front_banks(s, u)[0][c][:, :], ACT.Relu)\
                        .then_inc(hi_ready[s], 1)

            def project_qk(s, m):
                for w in range(2):
                    act.wait_ge(qk_ps[s], 2 * m + w + 1)
                    nc.scalar.activation(ST[s][:, w, m, 0, :], front_banks(s)[0][w][:, :], ACT.Copy)\
                        .then_inc(qk_hi[s], 1)

            def project_v(s):
                for i in range(2):
                    act.wait_ge(v_ps[s], i + 1)
                    nc.scalar.activation(V[s][:, 2 * i:2 * i + 2, :].rearrange("p t d -> p (t d)"), YB[i][:, :],
                                         ACT.Copy).then_inc(v_ready[s], 1)

            return rectified, project_qk, project_v

        def vector_parts(dve, free):
            v = nc.vector

            def masks(s):
                v.tensor_scalar(mask[s][:, :, :, :],
                                adj_stage[s].bitcast(I32).rearrange("p t (q j) -> p t j q", j=NT),
                                0.0, MASKED, ALU.is_equal, ALU.mult).then_inc(mask_ready[s], 1)
                dve.wait_ge(mask_ready[s], 1)
                v.tensor_copy(mask_self[s][:, :, :, :], mask[s][:, :, :, :]).then_inc(mask_ready[s], 1)

            def statistics(s, u, src):
                for t in range(NT):
                    v.bn_stats(stats[:, s, t, :], src[:, t, :]).then_inc(stat_done[s], 1)
                for t in range(NT):
                    dve.wait_ge(stat_done[s], 2 * NT * norm_no(s, u) + t + 1)
                    v.bn_aggr(mv[:, s, t, :], stats[:, s, t, :]).then_inc(stat_done[s], 1)
                dve.wait_ge(stat_done[s], 2 * NT * (norm_no(s, u) + 1))
                v.tensor_scalar(ve[:, s, :], mv[:, s, :, 1], EPS, None, ALU.add).then_inc(var_ready[s], 1)

            def norm(s, u, src, dst=Y):
                dve.wait_ge(rstd_ready[s], norm_no(s, u) + 1)
                if dst is Y:
                    free.wait("Y")
                for t in range(NT):
                    v.tensor_scalar(dst[:, t, :], src[:, t, :], mv[:, s, t, 0:1], rstd[:, s, t:t + 1],
                                    ALU.subtract, ALU.mult).then_inc(y_ready[s], 1)
                if u in TURN_OF:
                    n = ND * (turn_no(s, u) + 1)
                    if u in (2, 4, 6):
                        free.by("Y", (yT_ready[s], n), (res_ready[s], u - 1))
                    else:
                        free.by("Y", (yT_ready[s], n))

            def rectified(s, u):
                n = ND * turn_no(s, u)
                for c in range(ND):
                    dve.wait_ge(hi_ready[s], n + c + 1)
                    v.scalar_tensor_tensor(hT_lo[s][:, c, :], front_banks(s, u)[0][c][:, :], 0.0, hT_hi[s][:, c, :],
                                           ALU.max, ALU.subtract).then_inc(lo_ready[s], 1)

            def project_qk(s, m):
                for w in range(2):
                    dve.wait_ge(qk_hi[s], 2 * m + w + 1)
                    v.tensor_tensor(ST[s][:, w, m, 1, :], front_banks(s)[0][w][:, :], ST[s][:, w, m, 0, :], ALU.subtract)\
                        .then_inc(qk_lo[s], 1)

            return masks, statistics, norm, rectified, project_qk

        stage = [arena[:, 2048 * (i + 1):2048 * (i + 2)] for i in range(5)]
        b2_in = PR[:, 1, :, :].rearrange("p t n -> p (t n)")[:, 0:L1N * D].rearrange("p (l d) -> p l d", l=L1N)

        def bcast(src):
            return src.partition_broadcast(P)

        with nc.Block() as block:
            @block.sync
            def _(sp):
                blocks = [
                    [(w * 512, W.rearrange("(k p) n -> p k n", p=P)) for w, W in enumerate((Wq, Wk, Wv, Wo))],
                    [(w * 512, W.rearrange("(k p) n -> p k n", p=P)) for w, W in enumerate((L2W, L2attn, L3W))],
                ] + [[(0, W1[l].rearrange("(k p) n -> p k n", p=P))] for l in range(L1N)] \
                  + [[(0, W2[l].rearrange("(k p) n -> p k n", p=P))] for l in range(L1N)]
                fetch(sp, 0)
                for i, parts in enumerate(blocks):
                    if i >= len(stage):
                        sp.wait_ge(split, 2 * (i - len(stage) + 1))
                    for col, src in parts:
                        k, n = src.shape[1], src.shape[2]
                        sp.dma_start(stage[i % len(stage)][:, col:col + k * n].rearrange("p (k n) -> p k n", k=k), src)\
                          .then_inc(loaded[i], 16)
                bounce_out(sp, 0)
                sp.wait_ge(adj_in[1], 16)
                sp.wait_ge(bounced[0], 16 * 4)

            @block.scalar
            def _(act):
                def load(dst, src, small=False):
                    act.dma_start(dst, src, allow_slow_non_contiguous=small).then_inc(const_ready, 16)
                load(g1_bc[:, :, :], bcast(g1))
                load(res_bc[:, :, :], bcast(beta1))
                load(g2_bc[:, :, :], bcast(g2))
                load(beta2_bc[:, :, :], bcast(beta2))
                load(b2_in, bcast(b2))
                load(a_bc[:, 0:L1N, :, :], bcast(attn_w.rearrange("l (a d) -> l a d", a=2)))
                load(a_bc[:, L1N, :, :], bcast(L3a.rearrange("(a d) o -> a (d o)", a=2)))
                load(ab_bc[:, 0:L1N], bcast(attn_b))
                for c in range(ND):
                    load(g1_col[:, :, c], g1[:, c * P:c * P + P].rearrange("l p -> p l"), small=True)
                    load(beta1_col[:, :, c], beta1[:, c * P:c * P + P].rearrange("l p -> p l"), small=True)
                for l in range(L1N):
                    load(b1_col[:, l, :], b1[l].rearrange("(c p) -> p c", p=P), small=True)
                load(l2b_col[:, :], L2b.rearrange("(c p) -> p c", p=P), small=True)
                act.dma_start(X[1][:, :, :], x[1].rearrange("(p t) d -> p t d", t=NT)).then_inc(x_in[1], 16)
                rectified, project_qk, project_v = scalar_parts(act, Reader(act))
                rectified(0, BEFORE_LOOP)
                for m in range(2):
                    project_qk(0, m)
                project_v(0)
                act.wait_ge(const_ready, 16 * 16)
                act.wait_ge(x_in[1], 16)

            @block.gpsimd
            def _(pool):
                nc.gpsimd.memset(ident[:, :], 0.0).then_inc(ident_ready, 1)
                nc.gpsimd.memset(ones[:, :], 1.0).then_inc(ident_ready, 1)
                nc.gpsimd.memset(minus_half[:, :], -0.5).then_inc(ident_ready, 1)
                nc.gpsimd.memset(ab_bc[:, L1N:L1N + 1], 0.0).then_inc(ident_ready, 1)
                pool.wait_ge(ident_ready, 4)
                nc.gpsimd.affine_select(out=ident[:, :], in_=ident[:, :], compare_op=ALU.not_equal, fill=1.0,
                                        base=0, pattern=[[-1, P]], channel_multiplier=1).then_inc(ident_ready, 1)
                self_mask, norm = pool_parts(pool)
                norm(0, BEFORE_LOOP)
                self_mask(0)

            @block.tensor
            def _(pe):
                free = Reader(pe)
                mm3, turn, h_ready, hT, to_T, to_N, project_qk, project_v = tensor_parts(pe, free)
                pe.wait_ge(ident_ready, 5)
                turn(0, BEFORE_LOOP)
                h_ready(0, BEFORE_LOOP)
                pe.wait_ge(split, 2)
                for m in range(2):
                    project_qk(0, m)
                project_v(0)
                free.wait("U0")
                pe.wait_ge(loaded[W_TAIL], 16 * 3)
                for i in range(ND):
                    for o in range(ND):
                        last = nc.tensor.transpose(U[0][:, i * D + o * P:i * D + o * P + P],
                                                   stage[W_TAIL][:, o * D + i * P:o * D + i * P + P], ident[:, :])
                last.then_inc(wT, 1)

            @block.vector
            def _(dve):
                dmas = [4, 3, 1, 1, 1, 1, 1, 1]
                cols = [2048, 1536] + [2048] * 6
                masks, statistics, norm, rectified, project_qk = vector_parts(dve, Reader(dve))
                dve.wait_ge(x_in[0], 16)
                statistics(0, BEFORE_LOOP, X[0])
                norm(0, BEFORE_LOOP, X[0])
                rectified(0, BEFORE_LOOP)
                for i in range(NBLK):
                    if i == W_TAIL:
                        for m in range(2):
                            project_qk(0, m)
                        dve.wait_ge(adj_in[0], 16)
                        masks(0)
                    dve.wait_ge(loaded[i], 16 * dmas[i])
                    src = stage[i % len(stage)][:, 0:cols[i]]
                    first = 0
                    if i == W_TAIL:
                        dve.wait_ge(wT, 1)
                        nc.vector.tensor_copy(WH[:, i, 0:512], U[0][:, :]).then_inc(wT, 1)
                        dve.wait_ge(wT, 2)
                        nc.vector.tensor_tensor(WL[:, i, 0:512], U[0][:, :], WH[:, i, 0:512], ALU.subtract)\
                            .then_inc(wT, 1)
                        first = 512
                    nc.vector.tensor_copy(WH[:, i, first:cols[i]], src[:, first:]).then_inc(split, 1)
                    dve.wait_ge(split, 2 * i + 1)
                    nc.vector.tensor_tensor(WL[:, i, first:cols[i]], src[:, first:], WH[:, i, first:cols[i]],
                                            ALU.subtract).then_inc(split, 1)
                dve.wait_ge(const_ready, 16 * 16)
                nc.vector.tensor_tensor(res_bc[:, :, :], res_bc[:, :, :],
                                        b2_in, ALU.add).then_inc(split, 1)
        nc.all_engine_barrier(sems_to_clear=sems)

        with nc.Fori(0, B // STREAMS) as it:
            with nc.Block() as block:
                @block.sync
                def _(sp):
                    def bring(s, m):
                        for w, (stack, parts) in enumerate(((QS, (0, 0, 1)), (KS, (0, 1, 0)))):
                            for i, e in enumerate(parts):
                                sp.dma_start(stack[DK * i:DK * i + DK, HG * m:HG * m + HG, :],
                                             bounce[s, m, w, :, e, :].rearrange("(g r) n -> r g n", g=HG))\
                                  .then_inc(stack_in[m][s], 16)

                    for m in range(2):
                        bring(0, m)
                    bounce_out(sp, 1)
                    sp.wait_ge(bounced[1], 16 * 4)
                    for m in range(2):
                        sp.wait_ge(s0_ready[0], HG * NT * (m + 1))
                        bring(1, m)
                    sp.wait_ge(xs_ready[0], 3)
                    sp.dma_start(out[bass.ds(it * STREAMS, 1), :, :].rearrange("b (p t) d -> p (b t) d", t=NT),
                                 X[0][:, :, :]).then_inc(stored[0], 16)
                    sp.wait_ge(stored[0], 16)
                    fetch(sp, (it + 1) % (B // STREAMS))
                    bounce_out(sp, 0)
                    sp.wait_ge(adj_in[1], 16)
                    sp.wait_ge(bounced[0], 16 * 4)

                @block.gpsimd
                def _(pool):
                    def residual(s, l):
                        pool.wait_ge(y_ready[s], NT * (norm_no(s, 2 + 2 * l) + 1))
                        nc.gpsimd.tensor_tensor(RES[s][:, :, :], Y[:, :, :],
                                                g1_bc[:, l:l + 1, :].to_broadcast([P, NT, D]), ALU.mult)\
                            .then_inc(res_ready[s], 1)
                        pool.wait_ge(res_ready[s], 2 * l + 1)
                        nc.gpsimd.tensor_tensor(RES[s][:, :, :], RES[s][:, :, :],
                                                res_bc[:, l:l + 1, :].to_broadcast([P, NT, D]), ALU.add)\
                            .then_inc(res_ready[s], 1)

                    def heads():
                        for i in range(STREAMS * NH):
                            s, h = divmod(i, NH)
                            pool.wait_ge(r0_ready[s], h + 1)
                            for t in range(NT):
                                nc.gpsimd.tensor_scalar(PR[:, (i + 1) % 3, t, :], PR[:, (i + 1) % 3, t, :],
                                                        RINV[:, s, h, t:t + 1], 0.0, ALU.mult, ALU.add)\
                                    .then_inc(pn_ready[s], 1)
                            if i >= FIRST_WOVEN:
                                yield
                        yield from idle(LAST_HEAD_STEP + 2 - STREAMS * NH)

                    self_mask, norm = pool_parts(pool)
                    norm(1, 0)
                    self_mask(1)

                    def front():
                        norm(0, 0)
                        self_mask(0)
                        yield from idle(len(front_steps))

                    free = Reader(pool)

                    def forward(s, l):
                        for c in range(NC + 1):
                            if c:
                                n = NC * l + c - 1
                                pool.wait_ge(g_ready[s], 2 * n + 2)
                                free.wait(f"GL{n % 2}")
                                nc.gpsimd.tensor_tensor(GL[:, n % 2, :], GF[:, n % 2, :], GH[:, n % 2, :], ALU.subtract)\
                                    .then_inc(glo_ready[s], 1)
                                free.by(f"GL{n % 2}", (down_done[s], n + 1))
                            yield

                    def lower_x(s, n):
                        pool.wait_ge(xhi_ready[s], n + 1)
                        nc.gpsimd.tensor_tensor(XL[s][:, :, :], XN[s][:, :, :], XH[s][:, :, :], ALU.subtract)\
                            .then_inc(xlo_ready[s], 1)

                    def later(s):
                        norm(s, 1)
                        yield from idle(2)
                        for l in range(L1N):
                            lower_x(s, l)
                            yield from idle(len(rank1_steps) + len(tail_steps))
                            norm(s, 2 + 2 * l)
                            yield
                            residual(s, l)
                            yield from idle(1 + len(turn_steps))
                            yield from forward(s, l)
                            yield
                            norm(s, 3 + 2 * l)
                            yield from idle(2)
                        norm(s, 8)
                        yield from idle(2 + len(turn_steps) + len(dense_steps) + len(tail_steps) + len(elu_steps))
                        norm(s, 9)
                        yield from idle(2 + len(turn_steps) + 1 + len(rank1_steps) + len(tail_steps) + len(elu_steps))

                    weave(later, heads, front)

                @block.tensor
                def _(pe):
                    free = Reader(pe)

                    mm3, turn, h_ready, hT, to_T, to_N, project_qk, project_v = tensor_parts(pe, free)

                    def heads():
                        def score(i, t):
                            s, h = divmod(i, NH)
                            if h % HG == 0 and t == 0:
                                pe.wait_ge(stack_in[h // HG][s], 16 * 6)
                            free.wait(SCORE[t])
                            nc.tensor.matmul(SB4[t][:, :], QS[0:3 * DK, h, t * P:t * P + P], KS[0:3 * DK, h, :],
                                             start=True, stop=True).then_inc(s0_ready[s], 1)
                            free.by(SCORE[t], (z0_ready[s], h * NT + t + 1))

                        def turned(i, j):
                            s, h = divmod(i, NH)
                            if j == 0:
                                pe.wait_ge(pn_ready[s], NT * (h + 1))
                            free.wait(f"U{j % 2}")
                            for t in range(NT):
                                last = nc.tensor.transpose(U[j % 2][:, t * P:t * P + P],
                                                           PR[:, (i + 1) % 3, t, j * P:j * P + P], ident[:, :])
                            last.then_inc(pt0_ps[s], 1)
                            done = pt0_act if j % 2 == 0 else pt0_dve
                            free.by(f"U{j % 2}", (done[s], 2 * h + j // 2 + 1))

                        def weigh(group, j):
                            s, g = divmod(group, 2)
                            if j == 0:
                                free.wait(f"Y{g}")
                                if s:
                                    pe.wait_ge(v_ready[s], 2)
                            done = pt0_act if j % 2 == 0 else pt0_dve
                            pe.wait_ge(done[s], 2 * (HG * g + HG - 1) + j // 2 + 1)
                            for q in range(HG):
                                h = HG * g + q
                                last = nc.tensor.matmul(YB[g][DK * q:DK * q + DK, :], V[s][:, j, DK * h:DK * h + DK],
                                                        PT[:, q, j, :], start=(j == 0), stop=(j == NT - 1))
                            last.then_inc(pv_done[s], 1)
                            if j == NT - 1:
                                free.by(f"Y{g}", (o_lo[s], g + 1))

                        def output(s, t):
                            if t == 0:
                                pe.wait_ge(o_lo[s], 2)
                            if t % 2 == 0:
                                free.wait(f"Y{t // 2}")
                            for g in range(2):
                                c = slice(t * P, t * P + P)
                                last = mm3(YB[t // 2][:, (t % 2) * D:(t % 2) * D + D], hT_hi[s][:, g, c], hT_lo[s][:, g, c],
                                           wblk(WH, W_L0, 3, g, 0, D), wblk(WL, W_L0, 3, g, 0, D),
                                           g == 0 and t % 2 == 0, g == 1)
                            if t % 2:
                                last.then_inc(wo_done[s], 1)
                                free.by(f"Y{t // 2}", (x1_ready[s], t // 2 + 1))

                        for t in range(NT):
                            score(0, t)
                        for i in range(LAST_HEAD_STEP + 1):
                            for j in range(NT):
                                if (i, j) == (1, 0):
                                    turn(1, 0)
                                if i in WEIGHED_AT:
                                    weigh(WEIGHED_AT.index(i), j)
                                if i == OUTPUT_AT:
                                    output(0, j)
                                if 2 <= i < STREAMS * NH + 2:
                                    turned(i - 2, j)
                                if i + 1 < STREAMS * NH:
                                    score(i + 1, j)
                            if i == 1:
                                h_ready(1, 0)
                            if i in (1, 2):
                                project_qk(1, i - 1)
                            if i == 3:
                                project_v(1)
                            if i >= FIRST_WOVEN:
                                yield
                        for t in range(NT):
                            output(1, t)
                        yield

                    def row_scores(s, use):
                        n = use if use < USE_L2 else 3
                        pe.wait_ge(diag_ready[s], NT * (n + 1))
                        free.wait("P0")
                        nc.tensor.matmul(PB[0][:, :], ones[:, :], diag[:, :, :].rearrange("p t n -> p (t n)"),
                                         start=True, stop=True).then_inc(sj_ready[s], 1)
                        free.by("P0", (z_ready[s], NT * (use + 1)))

                    def tail(s, use):
                        def turned(j):
                            free.wait(f"P{j % 2}")
                            for t in range(NT):
                                last = nc.tensor.transpose(PB[j % 2][:, t * P:t * P + P], PR[:, s, t, j * P:j * P + P],
                                                           ident[:, :])
                            last.then_inc(pt_ps[s], 1)
                            free.by(f"P{j % 2}", (pt_lo[s], NT * use + j + 1))

                        def weigh(j):
                            if j == 0:
                                free.wait("G0")
                                free.wait("G1")
                                pe.wait_ge(xlo_ready[s], use + 1)
                            pe.wait_ge(pt_lo[s], NT * use + j + 1)
                            for t in range(NT):
                                c = slice(t * P, t * P + P)
                                last = mm3(GB[t // 2][:, (t % 2) * D:(t % 2) * D + D], PTH[:, j, c], PTL[:, j, c],
                                           XH[s][:, j, :], XL[s][:, j, :], j == 0 and t % 2 == 0, j == NT - 1)
                                if j == NT - 1 and t % 2:
                                    last.then_inc(agg_ps[s], 1)

                        pe.wait_ge(p_ready[s], NT * (use + 1))
                        for i in range(NT + 2):
                            if i < NT:
                                turned(i)
                            if i >= 2:
                                weigh(i - 2)
                            if i == NT + 1:
                                for t in (1, 3):
                                    free.by(f"G{t // 2}", (src_ready[s], 2 * NT * use + t + 1) if use < USE_L2
                                            else (hp_ready[s], NT * (use - USE_L2) + t + 1))
                            yield

                    def forward(s, l):
                        def up(c):
                            free.wait(f"U{c % 2}")
                            for k in range(ND):
                                w = slice(k * HID + c * P, k * HID + c * P + P)
                                last = mm3(U[c % 2][:, :], WH[:, W_UP + l, w], WL[:, W_UP + l, w], *hT(s, k),
                                           k == 0, k == ND - 1)
                            last.then_inc(up_ps[s], 1)
                            free.by(f"U{c % 2}", (g_ready[s], 2 * (NC * l + c + 1)))

                        def down(c):
                            if c == 0:
                                free.wait("Y0")
                                free.wait("Y1")
                            pe.wait_ge(g_ready[s], 2 * (NC * l + c + 1))
                            pe.wait_ge(glo_ready[s], NC * l + c + 1)
                            w = slice(c * D, c * D + D)
                            for t in range(NT):
                                g = slice(t * P, t * P + P)
                                last = mm3(YB[t // 2][:, (t % 2) * D:(t % 2) * D + D], GH[:, c % 2, g], GL[:, c % 2, g],
                                           WH[:, W_DOWN + l, w], WL[:, W_DOWN + l, w], c == 0 and t % 2 == 0, c == NC - 1)
                            last.then_inc(down_done[s], 1)

                        h_ready(s, 2 + 2 * l)
                        for c in range(NC + 2):
                            if c < NC:
                                up(c)
                            if c >= 2:
                                down(c - 2)
                            if c == NC + 1:
                                for i in range(2):
                                    free.by(f"Y{i}", (src_ready[s], 2 * NT * (l + 1)))
                            yield
                        yield
                        yield

                    def dense(s):
                        h_ready(s, 8)
                        for m in range(ND):
                            free.wait(f"U{m}")
                            to_T(U[m], s, W_TAIL, 0, m).then_inc(h2_ps[s], 1)
                            free.by(f"U{m}", (h2_f[s], 2 * (m + 1)))
                        yield
                        pe.wait_ge(h2_f[s], 2 * ND)
                        for t in range(NT):
                            if t % 2 == 0:
                                free.wait(f"G{t // 2}")
                            for c in range(ND):
                                last = nc.tensor.transpose(GB[t // 2][:, (t % 2) * D + c * P:(t % 2) * D + c * P + P],
                                                           tT[:, c, t * P:t * P + P], ident[:, :])
                            if t % 2:
                                last.then_inc(hn_ps[s], 1)
                                free.by(f"G{t // 2}", (xlo_ready[s], USE_L2 + 1))
                        yield
                        pe.wait_ge(h2_lo[s], ND)
                        for m in range(ND):
                            free.wait(f"U{m}")
                            for k in range(ND):
                                last = mm3(U[m][:, :], wblk(WH, W_TAIL, 1, k, m * P, P), wblk(WL, W_TAIL, 1, k, m * P, P),
                                           *hT(s, k), k == 0, k == ND - 1)
                            last.then_inc(ha_ps[s], 1)
                            free.by(f"U{m}", (ha_lo[s], m + 1))
                        yield
                        pe.wait_ge(ha_lo[s], ND)
                        for t in range(NT):
                            free.wait(SCORE[t])
                            c = slice(t * P, t * P + P)
                            for k in range(ND):
                                last = mm3(SB4[t][:, :], HAH[:, k, c], HAL[:, k, c], *hT(s, k), k == 0, k == ND - 1)
                            last.then_inc(s2_ps[s], 1)
                            free.by(SCORE[t], (z_ready[s], NT * USE_L2 + t + 1))
                            if t % 2:
                                yield
                        yield

                    def wh(s):
                        h_ready(s, 9)
                        for i, last in enumerate(to_N(GB, "G", s, W_TAIL, 2)):
                            last.then_inc(hn_ps[s], 1)
                            free.by(f"G{i}", (xlo_ready[s], USE_L3 + 1))
                        yield

                    def rank1(s, use):
                        yield
                        row_scores(s, use)
                        yield from idle(len(rank1_steps) - 1)

                    def turned(s, u):
                        yield from idle(2)
                        turn(s, u)
                        yield from idle(2)

                    def later(s):
                        yield from idle(2)
                        for l in range(L1N):
                            yield from rank1(s, l)
                            yield from tail(s, l)
                            yield from turned(s, 2 + 2 * l)
                            yield from forward(s, l)
                        yield from turned(s, 8)
                        yield from dense(s)
                        yield from tail(s, USE_L2)
                        yield from idle(2)
                        yield from turned(s, 9)
                        yield from wh(s)
                        yield from rank1(s, USE_L3)
                        yield from tail(s, USE_L3)
                        yield from idle(2)

                    def front():
                        yield from idle(2)
                        turn(0, 0)
                        yield from idle(2)
                        h_ready(0, 0)
                        for m in range(2):
                            project_qk(0, m)
                            yield
                        project_v(0)
                        yield

                    weave(later, heads, front)

                @block.scalar
                def _(act):
                    free = Reader(act)
                    rectified, project_qk, project_v = scalar_parts(act, free)

                    def scaled(s, l):
                        v = turn_no(s, 2 + 2 * l)
                        free.wait(f"hT{s}")
                        free.wait("tT")
                        for c in range(ND):
                            act.wait_ge(yT_ready[s], ND * v + c + 1)
                            for dst, done in ((tT, t_ready), (hT_hi[s], hi_ready)):
                                nc.scalar.activation(dst[:, c, :], U[c][:, :], ACT.Identity, bias=beta1_col[:, l, c:c + 1],
                                                     scale=g1_col[:, l, c:c + 1]).then_inc(done[s], 1)
                        free.by("tT", (lo_ready[s], ND * v + ND))
                        free.by(f"hT{s}", (down_done[s], NC * (l + 1)))

                    def heads():
                        def place_free(i):
                            s, h = divmod(i - 3, NH)
                            act.wait_ge(pt0_ps[s], NT * (h + 1))

                        for i in range(LAST_HEAD_STEP + 1):
                            s, h = divmod(i, NH)
                            for t in range(NT):
                                if i < STREAMS * NH:
                                    if i >= 3 and t == 0:
                                        place_free(i)
                                    act.wait_ge(z0_ready[s], h * NT + t + 1)
                                    nc.scalar.activation(PR[:, (i + 1) % 3, t, :], Z[:, t, :], ACT.Exp, scale=-1.0,
                                                         bias=NMIN[:, s, h, t:t + 1],
                                                         accum_out=RSUM[:, s, h, t:t + 1]).then_inc(p0_ready[s], 1)
                                if 2 <= i < STREAMS * NH + 2 and t % 2 == 0:
                                    evacuate(act, i - 2, t)
                                    u, g = divmod(i - 2, NH)
                                    nc.scalar.activation(PT[:, g % HG, t, :], U[0][:, :], ACT.Copy)\
                                        .then_inc(pt0_act[u], 1)
                                if (i, t) == (1, 0):
                                    rectified(1, 0)
                                if (i, t) in ((2, 0), (3, 0)):
                                    project_qk(1, i - 2)
                                if (i, t) == (4, 0):
                                    project_v(1)
                            if i in WEIGHED_AT:
                                u, g = divmod(WEIGHED_AT.index(i), 2)
                                act.wait_ge(pv_done[u], NT * (g + 1))
                                nc.scalar.activation(hT_hi[u][:, g, :], YB[g][:, :], ACT.Relu).then_inc(o_hi[u], 1)
                                if i == WEIGHED_AT[1]:
                                    free.by("hT0", (wo_done[0], 2))
                            if i >= FIRST_WOVEN:
                                yield
                        free.by("hT1", (wo_done[1], 2))
                        yield

                    def upper_x(s, n):
                        act.wait_ge(xn_ready[s], n + 1)
                        if n:
                            act.wait_ge(agg_ps[s], 2 * n)
                        nc.scalar.activation(XH[s][:, :, :], XN[s][:, :, :], ACT.Copy).then_inc(xhi_ready[s], 1)

                    def rank1(s, use):
                        n = use if use < USE_L2 else 3
                        yield from idle(2)
                        act.wait_ge(small_done[s], 5 * n + 2)
                        for t in range(NT):
                            act.wait_ge(z_ready[s], NT * use + t + 1)
                            nc.scalar.activation(PR[:, s, t, :], ZS[s][:, t, :], ACT.Relu, scale=1.0 - SLOPE,
                                                 bias=eb[:, s, 0, t:t + 1]).then_inc(relu_ready[s], 1)
                            if t % 2:
                                yield
                        yield
                        act.wait_ge(small_ready[s], n + 1)
                        for t in range(NT):
                            act.wait_ge(w_ready[s], NT * n + t + 1)
                            nc.scalar.activation(PR[:, s, t, :], ZS[s][:, t, :], ACT.Exp, bias=eb[:, s, 1, t:t + 1],
                                                 accum_out=RSUM[:, s, 0, t:t + 1]).then_inc(p_ready[s], 1)
                        yield

                    def tail(s, use):
                        free.wait("PTH")
                        for j in range(NT):
                            act.wait_ge(pt_ps[s], NT * use + j + 1)
                            nc.scalar.activation(PTH[:, j, :], PB[j % 2][:, :], ACT.Copy).then_inc(pt_hi[s], 1)
                            yield
                        free.by("PTH", (agg_ps[s], 2 * (use + 1)))
                        yield from idle(2)

                    def forward(s, l):
                        for c in range(NC):
                            n = NC * l + c
                            act.wait_ge(up_ps[s], n + 1)
                            free.wait(f"GF{c % 2}")
                            for dst in (GF, GH):
                                nc.scalar.activation(dst[:, c % 2, :], U[c % 2][:, :], ACT.Gelu,
                                                     bias=b1_col[:, l, c:c + 1]).then_inc(g_ready[s], 1)
                            free.by(f"GF{c % 2}", (down_done[s], n + 1))
                            yield
                        yield from idle(4)

                    def dense(s):
                        free.wait("tT")
                        free.wait(f"hT{s}")
                        for m in range(ND):
                            act.wait_ge(h2_ps[s], ND)
                            for dst in (tT, hT_hi[s]):
                                nc.scalar.activation(dst[:, m, :], U[m][:, :], ACT.Identity, bias=l2b_col[:, m:m + 1])\
                                    .then_inc(h2_f[s], 1)
                        free.by("tT", (h2_lo[s], ND), (hn_ps[s], 2))
                        free.by(f"hT{s}", (s2_ps[s], NT))
                        yield
                        for i in range(2):
                            act.wait_ge(hn_ps[s], i + 1)
                            nc.scalar.activation(XH[s][:, 2 * i:2 * i + 2, :].rearrange("p t d -> p (t d)"), GB[i][:, :],
                                                 ACT.Copy).then_inc(xhi_ready[s], 1)
                        yield
                        for m in range(ND):
                            act.wait_ge(ha_ps[s], m + 1)
                            nc.scalar.activation(HAH[:, m, :], U[m][:, :], ACT.Copy).then_inc(ha_hi[s], 1)
                        yield
                        yield
                        for t in range(NT):
                            act.wait_ge(z_ready[s], NT * USE_L2 + t + 1)
                            nc.scalar.activation(PR[:, s, t, :], ZS[s][:, t, :], ACT.Exp, scale=-1.0,
                                                 bias=NMIN[:, s, 0, t:t + 1],
                                                 accum_out=RSUM[:, s, 0, t:t + 1]).then_inc(p_ready[s], 1)
                            if t % 2:
                                yield

                    def wh(s):
                        for i in range(2):
                            act.wait_ge(hn_ps[s], 3 + i)
                            for dst, done in ((XN[s], xn_ready), (XH[s], xhi_ready)):
                                nc.scalar.activation(dst[:, 2 * i:2 * i + 2, :].rearrange("p t d -> p (t d)"),
                                                     GB[i][:, :], ACT.Copy).then_inc(done[s], 1)
                        free.by(f"hT{s}", (hn_ps[s], 4))
                        yield

                    def elu(s, i):
                        act.wait_ge(mn_ready[s], i + 1)
                        nc.scalar.activation(RES[s][:, :, :], RES[s][:, :, :], ACT.Exp).then_inc(ex_ready[s], 1)
                        yield from idle(2)

                    def later(s):
                        yield from idle(2)
                        for l in range(L1N):
                            upper_x(s, l)
                            yield from rank1(s, l)
                            yield from tail(s, l)
                            yield from idle(2)
                            scaled(s, l)
                            yield from idle(2)
                            yield from forward(s, l)
                        yield from idle(2)
                        rectified(s, 8)
                        free.by(f"hT{s}", (h2_ps[s], ND))
                        yield from idle(2)
                        yield from dense(s)
                        yield from tail(s, USE_L2)
                        yield from elu(s, 0)
                        yield from idle(2)
                        rectified(s, 9)
                        yield from idle(2)
                        yield from wh(s)
                        yield from rank1(s, USE_L3)
                        yield from tail(s, USE_L3)
                        yield from elu(s, 1)

                    def front():
                        yield from idle(2)
                        rectified(0, 0)
                        yield from idle(2)
                        free.wait("GF0")
                        free.wait("GF1")
                        for m in range(2):
                            project_qk(0, m)
                            yield
                        free.wait("tT")
                        project_v(0)
                        yield

                    store_second(act, (it + B // STREAMS - 1) % (B // STREAMS))
                    act.dma_start(X[1][:, :, :],
                                  x[bass.ds(it * STREAMS + 1, 1), :, :].rearrange("b (p t) d -> p (b t) d", t=NT))\
                       .then_inc(x_in[1], 16)
                    weave(later, heads, front)

                @block.vector
                def _(dve):
                    free = Reader(dve)
                    v = nc.vector
                    masks, statistics, norm, rectified, project_qk = vector_parts(dve, free)

                    def scaled(s, l):
                        n = ND * turn_no(s, 2 + 2 * l)
                        for c in range(ND):
                            dve.wait_ge(hi_ready[s], n + c + 1)
                            dve.wait_ge(t_ready[s], ND * l + c + 1)
                            v.tensor_tensor(hT_lo[s][:, c, :], tT[:, c, :], hT_hi[s][:, c, :], ALU.subtract)\
                                .then_inc(lo_ready[s], 1)

                    def heads():
                        masks(1)
                        for i in range(LAST_HEAD_STEP + 1):
                            s, h = divmod(i, NH)
                            for t in range(NT):
                                if i < STREAMS * NH:
                                    dve.wait_ge(s0_ready[s], h * NT + t + 1)
                                    if i:
                                        u, g = divmod(i - 1, NH)
                                        dve.wait_ge(p0_ready[u], g * NT + t + 1)
                                    v.tensor_tensor_reduce(
                                        out=Z[:, t, :], in0=SB4[t][:, :],
                                        in1=mask[s][:, t, :, :].rearrange("p j q -> p (j q)"), scale=NEG_SCALE,
                                        scalar=3e38, op0=ALU.add, op1=ALU.min,
                                        accum_out=NMIN[:, s, h, t:t + 1]).then_inc(z0_ready[s], 1)
                                if t == 1 and 1 <= i <= STREAMS * NH:
                                    u, g = divmod(i - 1, NH)
                                    dve.wait_ge(p0_ready[u], NT * (g + 1))
                                    v.reciprocal(RINV[:, u, g, :], RSUM[:, u, g, :]).then_inc(r0_ready[u], 1)
                                if 2 <= i < STREAMS * NH + 2 and t % 2:
                                    evacuate(dve, i - 2, t)
                                    u, g = divmod(i - 2, NH)
                                    v.tensor_copy(PT[:, g % HG, t, :], U[1][:, :]).then_inc(pt0_dve[u], 1)
                            if i in WEIGHED_AT:
                                u, g = divmod(WEIGHED_AT.index(i), 2)
                                dve.wait_ge(o_hi[u], g + 1)
                                v.scalar_tensor_tensor(hT_lo[u][:, g, :], YB[g][:, :], 0.0, hT_hi[u][:, g, :],
                                                       ALU.max, ALU.subtract).then_inc(o_lo[u], 1)
                            if i == 0:
                                dve.wait_ge(x_in[1], 16)
                                statistics(1, 0, X[1])
                                norm(1, 0, X[1])
                            if i == 1:
                                rectified(1, 0)
                            if i in (2, 3):
                                project_qk(1, i - 2)
                            if i == OUTPUT_AT:
                                add_output(0)
                            if i >= FIRST_WOVEN:
                                yield
                        add_output(1)
                        yield

                    def add_output(s):
                        for i in range(2):
                            dve.wait_ge(wo_done[s], i + 1)
                            xs = X[s][:, 2 * i:2 * i + 2, :].rearrange("p t d -> p (t d)")
                            v.tensor_tensor(xs, xs, YB[i][:, :], ALU.add).then_inc(x1_ready[s], 1)

                    def rank1(s, use):
                        n = use if use < USE_L2 else 3
                        k = 5 * n
                        si, sj, c, top, u1, u2 = (sml[:, s, i, :] for i in range(6))
                        dve.wait_ge(xn_ready[s], use + 1 if use < USE_L2 else L1N + 3)
                        for t in range(NT):
                            for dst, a in ((sj, 1), (si, 0)):
                                v.tensor_tensor_reduce(out=ZS[s][:, t, a * D:a * D + D], in0=XN[s][:, t, :],
                                                       in1=a_bc[:, n, a, :], scale=1.0, scalar=0.0, op0=ALU.mult,
                                                       op1=ALU.add, accum_out=dst[:, t:t + 1]).then_inc(dot_done[s], 1)
                            if t == 1:
                                yield
                        free.wait("diag")
                        for t in range(NT):
                            dve.wait_ge(dot_done[s], 2 * NT * n + 2 * t + 2)
                            v.tensor_scalar(diag[:, t, :], ident[:, :], sj[:, t:t + 1], None, ALU.mult)\
                                .then_inc(diag_ready[s], 1)
                        free.by("diag", (sj_ready[s], n + 1))
                        v.tensor_scalar(c, si, ab_bc[:, n:n + 1], None, ALU.add).then_inc(small_done[s], 1)
                        dve.wait_ge(small_done[s], k + 1)
                        v.tensor_scalar(eb[:, s, 0, :], c, 1.0 - SLOPE, None, ALU.mult).then_inc(small_done[s], 1)
                        yield
                        m = mask_self if use < USE_L2 else mask
                        if use < USE_L2 and s:
                            dve.wait_ge(self_ready[s], NT)
                        dve.wait_ge(sj_ready[s], n + 1)
                        for t in range(NT):
                            v.tensor_tensor_reduce(out=ZS[s][:, t, :], in0=PB[0][:, :],
                                                   in1=m[s][:, t, :, :].rearrange("p j q -> p (j q)"), scale=1.0,
                                                   scalar=-3e38, op0=ALU.add, op1=ALU.max,
                                                   accum_out=top[:, t:t + 1]).then_inc(z_ready[s], 1)
                            if t == 1:
                                yield
                        dve.wait_ge(z_ready[s], NT * (use + 1))
                        v.tensor_tensor(u1, top, c, ALU.add).then_inc(small_done[s], 1)
                        dve.wait_ge(small_done[s], k + 3)
                        v.scalar_tensor_tensor(u2, u1, SLOPE, u1, ALU.mult, ALU.max).then_inc(small_done[s], 1)
                        dve.wait_ge(small_done[s], k + 4)
                        v.scalar_tensor_tensor(eb[:, s, 1, :], c, SLOPE, u2, ALU.mult, ALU.subtract)\
                            .then_inc(small_done[s], 1)
                        dve.wait_ge(small_done[s], k + 5)
                        v.tensor_copy(sml[:, s, 7, :], eb[:, s, 1, :]).then_inc(small_ready[s], 1)
                        yield
                        for t in range(NT):
                            dve.wait_ge(relu_ready[s], NT * n + t + 1)
                            v.scalar_tensor_tensor(ZS[s][:, t, :], ZS[s][:, t, :], SLOPE, PR[:, s, t, :],
                                                   ALU.mult, ALU.add).then_inc(w_ready[s], 1)
                            if t % 2:
                                yield

                    def tail(s, use, taken):
                        yield
                        for j in range(NT):
                            dve.wait_ge(pt_hi[s], NT * use + j + 1)
                            v.tensor_tensor(PTL[:, j, :], PB[j % 2][:, :], PTH[:, j, :], ALU.subtract)\
                                .then_inc(pt_lo[s], 1)
                            if j == NT - 1:
                                dve.wait_ge(p_ready[s], NT * (use + 1))
                                v.reciprocal(RINV[:, s, 0, :], RSUM[:, s, 0, :]).then_inc(rinv_ready[s], 1)
                            yield
                        dve.wait_ge(rinv_ready[s], use + 1)
                        taken(0)
                        yield

                    def aggregated(s, l):
                        def half(i):
                            dve.wait_ge(agg_ps[s], 2 * l + i + 1)
                            for t in (2 * i, 2 * i + 1):
                                v.scalar_tensor_tensor(XN[s][:, t, :], GB[i][:, (t % 2) * D:(t % 2) * D + D],
                                                       RINV[:, s, 0, t:t + 1], XN[s][:, t, :], ALU.mult, ALU.add)\
                                    .then_inc(src_ready[s], 1)
                        return half

                    def forward(s, l):
                        yield from idle(NC + 2)
                        dve.wait_ge(down_done[s], NC * (l + 1))
                        dve.wait_ge(res_ready[s], 2 * l + 2)
                        for t in range(NT):
                            v.tensor_tensor(XN[s][:, t, :], YB[t // 2][:, (t % 2) * D:(t % 2) * D + D], RES[s][:, t, :],
                                            ALU.add).then_inc(src_ready[s], 1)
                        dve.wait_ge(src_ready[s], 2 * NT * l + 2 * NT)
                        statistics(s, 3 + 2 * l, XN[s])
                        yield
                        norm(s, 3 + 2 * l, XN[s])
                        dve.wait_ge(y_ready[s], NT * (norm_no(s, 3 + 2 * l) + 1))
                        v.tensor_tensor(XN[s][:, :, :], Y[:, :, :], g2_bc[:, l:l + 1, :].to_broadcast([P, NT, D]),
                                        ALU.mult).then_inc(half_done[s], 1)
                        dve.wait_ge(half_done[s], l + 1)
                        v.tensor_tensor(XN[s][:, :, :], XN[s][:, :, :], beta2_bc[:, l:l + 1, :].to_broadcast([P, NT, D]),
                                        ALU.add).then_inc(xn_ready[s], 1)
                        if l == L1N - 1:
                            dve.wait_ge(xn_ready[s], L1N + 1)
                            v.tensor_tensor(X[s][:, :, :], X[s][:, :, :], XN[s][:, :, :], ALU.add)\
                                .then_inc(xs_ready[s], 1)
                        yield

                    def lower_x(s, n):
                        for i in range(2):
                            dve.wait_ge(xhi_ready[s], n + i + 1)
                            c = slice(2 * i, 2 * i + 2)
                            last = v.tensor_tensor(XL[s][:, c, :].rearrange("p t d -> p (t d)"), GB[i][:, :],
                                                   XH[s][:, c, :].rearrange("p t d -> p (t d)"), ALU.subtract)
                        last.then_inc(xlo_ready[s], 1)

                    def dense(s):
                        yield
                        for m in range(ND):
                            dve.wait_ge(h2_f[s], 2 * (m + 1))
                            v.tensor_tensor(hT_lo[s][:, m, :], tT[:, m, :], hT_hi[s][:, m, :], ALU.subtract)\
                                .then_inc(h2_lo[s], 1)
                        yield
                        lower_x(s, L1N)
                        yield
                        for m in range(ND):
                            dve.wait_ge(ha_hi[s], m + 1)
                            v.tensor_tensor(HAL[:, m, :], U[m][:, :], HAH[:, m, :], ALU.subtract).then_inc(ha_lo[s], 1)
                        yield
                        for t in range(NT):
                            dve.wait_ge(s2_ps[s], t + 1)
                            v.tensor_tensor_reduce(out=ZS[s][:, t, :], in0=SB4[t][:, :],
                                                   in1=mask[s][:, t, :, :].rearrange("p j q -> p (j q)"), scale=-1.0,
                                                   scalar=3e38, op0=ALU.add, op1=ALU.min,
                                                   accum_out=NMIN[:, s, 0, t:t + 1]).then_inc(z_ready[s], 1)
                            if t % 2:
                                yield

                    def scaled_out(s, i):
                        def half(k):
                            dve.wait_ge(agg_ps[s], 2 * (USE_L2 + i) + k + 1)
                            for t in (2 * k, 2 * k + 1):
                                v.tensor_scalar(XN[s][:, t, :], GB[k][:, (t % 2) * D:(t % 2) * D + D],
                                                RINV[:, s, 0, t:t + 1], None, ALU.mult).then_inc(hp_ready[s], 1)
                        return half

                    def elu(s, i):
                        scaled_out(s, i)(1)
                        dve.wait_ge(hp_ready[s], NT * (i + 1))
                        v.tensor_scalar(RES[s][:, :, :], XN[s][:, :, :], 0.0, None, ALU.min).then_inc(mn_ready[s], 1)
                        yield
                        dve.wait_ge(ex_ready[s], i + 1)
                        v.scalar_tensor_tensor(XN[s][:, :, :], XN[s][:, :, :], 0.0, RES[s][:, :, :], ALU.max, ALU.add)\
                            .then_inc(el_ready[s], 1)
                        dve.wait_ge(el_ready[s], i + 1)
                        v.scalar_tensor_tensor(X[s][:, :, :], XN[s][:, :, :], -1.0, X[s][:, :, :], ALU.add, ALU.add)\
                            .then_inc(xs_ready[s], 1)
                        yield

                    def enter(s, u, ready, n):
                        dve.wait_ge(ready[s], n)
                        statistics(s, u, X[s])
                        yield
                        norm(s, u, X[s])
                        yield
                        if u in TURN_OF:
                            yield
                            rectified(s, u)
                            yield

                    def later(s):
                        dve.wait_ge(x1_ready[s], 2)
                        statistics(s, 1, X[s])
                        yield
                        norm(s, 1, X[s], XN[s])
                        dve.wait_ge(y_ready[s], NT * (norm_no(s, 1) + 1))
                        v.tensor_scalar(XN[s][:, :, :], XN[s][:, :, :], 0.0, None, ALU.max).then_inc(xn_ready[s], 1)
                        yield
                        for l in range(L1N):
                            yield from rank1(s, l)
                            yield from tail(s, l, aggregated(s, l))
                            aggregated(s, l)(1)
                            dve.wait_ge(src_ready[s], 2 * NT * l + NT)
                            statistics(s, 2 + 2 * l, XN[s])
                            yield
                            norm(s, 2 + 2 * l, XN[s])
                            yield
                            yield
                            scaled(s, l)
                            yield
                            yield from forward(s, l)
                        yield from enter(s, 8, xs_ready, 1)
                        yield from dense(s)
                        yield from tail(s, USE_L2, scaled_out(s, 0))
                        yield from elu(s, 0)
                        yield from enter(s, 9, xs_ready, 2)
                        yield
                        lower_x(s, L1N + 2)
                        yield from rank1(s, USE_L3)
                        yield from tail(s, USE_L3, scaled_out(s, 1))
                        yield from elu(s, 1)

                    def front():
                        dve.wait_ge(x_in[0], 16)
                        statistics(0, 0, X[0])
                        dve.wait_ge(adj_in[0], 16)
                        masks(0)
                        yield
                        norm(0, 0, X[0])
                        yield from idle(2)
                        rectified(0, 0)
                        yield
                        for m in range(2):
                            project_qk(0, m)
                            yield
                        yield

                    weave(later, heads, front)
            nc.all_engine_barrier(sems_to_clear=sems)

        with nc.Block() as block:
            @block.sync
            def _(sp):
                store_second(sp, B // STREAMS - 1)


_INS = ["x", "adj", "L0_gnn_Wq", "L0_gnn_Wk", "L0_gnn_Wv", "L0_gnn_Wo", "L1_gnn_attn_w", "L1_gnn_attn_b",
        "L1_gnn_W1", "L1_gnn_b1", "L1_gnn_W2", "L1_gnn_b2", "L1_gnn_g1", "L1_gnn_beta1", "L1_gnn_g2",
        "L1_gnn_beta2", "L2_gnn_W", "L2_gnn_b", "L2_gnn_attn", "L3_gnn_W", "L3_gnn_a"]


def kernel(**inputs):
    import numpy as np
    import concourse.bacc as bacc
    from concourse.bass_utils import run_bass_kernel_spmd

    nc = bacc.Bacc("TRN2", target_bir_lowering=False, num_devices=1)
    arrays, args = {}, []
    for name in _INS:
        a = np.ascontiguousarray(inputs[name])
        arrays[f"in_{name}"] = a
        args.append(nc.dram_tensor(f"in_{name}", a.shape, mybir.dt.from_np(a.dtype), kind="ExternalInput").ap())
    args.append(nc.dram_tensor("out", (B, N, D), F32, kind="ExternalOutput").ap())
    build(nc, *args)
    r = run_bass_kernel_spmd(nc, [arrays], core_ids=[0])
    return r.results[0]["out"]
```
